# Optimizing a Trainium2 kernel written in Bass

```python
import numpy as np
import jax
import jax.numpy as jnp

def _softmax(x, axis=-1):
    return jax.nn.softmax(x, axis=axis)

def _gelu(x):
    return jax.nn.gelu(x, approximate=True)

def _silu(x):
    return jax.nn.silu(x)

def _sigmoid(x):
    return jax.nn.sigmoid(x)

def _layernorm(x, axis=-1, eps=1e-05):
    m = jnp.mean(x, axis=axis, keepdims=True)
    v = jnp.var(x, axis=axis, keepdims=True)
    return (x - m) / jnp.sqrt(v + eps)

def _scatter_add(tgt, idx, src, axis=0):
    return tgt.at[idx].add(src)

def _segment_sum(src, seg, n):
    return jax.ops.segment_sum(src, seg, n)
kernel_name = 'mk_adj_resnorm_d2_adj_r2_3fe8a7'

def setup_inputs(seed: int=0):
    np.random.seed(seed)
    _w = jnp.asarray

    def _rec_inputs():
        import jax
        import jax.numpy as jnp
        _gk = jax.random.key(seed)
        x = -0.0002928 + 1 * jax.random.normal(jax.random.fold_in(_gk, 1), (8, 1024, 256), jnp.float32)
        _a = jax.random.bernoulli(jax.random.fold_in(_gk, 2), 0.015625, (8, 1024, 1024))
        _a = jnp.logical_or(_a, jnp.swapaxes(_a, -1, -2))
        _a = jnp.logical_or(_a, jnp.eye(1024, dtype=bool))
        _af = _a.astype(jnp.float32)
        _af = _af * jax.random.uniform(jax.random.fold_in(_gk, 3), (8, 1024, 1024), jnp.float32, 0.05, 1)
        adj = _af
        return (x, adj)
    x, adj = _rec_inputs()

    def _L0_gnn_setup():
        import jax, jax.numpy as jnp
        import numpy as np
        B, N, DIN, DOUT, K = (4, 1024, 256, 256, 3)
        key = jax.random.key(seed)
        ks = jax.random.split(key, 8)
        X = jax.random.normal(ks[0], (B, N, DIN), dtype=jnp.float32)
        A = jax.random.uniform(ks[1], (B, N, N), dtype=jnp.float32)
        Wv = jax.random.normal(ks[2], (DIN, DOUT), dtype=jnp.float32) * 0.02
        bv = jax.random.normal(ks[3], (DOUT,), dtype=jnp.float32) * 0.02
        aw = jax.random.normal(ks[4], (2 * DOUT, 1), dtype=jnp.float32) * 0.05
        ab = jax.random.normal(ks[5], (1,), dtype=jnp.float32) * 0.05
        Wk = jax.random.normal(ks[6], (K, DIN, DOUT), dtype=jnp.float32) * 0.02
        bk = jax.random.normal(ks[7], (K, DOUT), dtype=jnp.float32) * 0.02
        return {'X': X, 'A': A, 'Wv': Wv, 'bv': bv, 'aw': aw, 'ab': ab, 'Wk': Wk, 'bk': bk}
    _L0_gnn_all = _L0_gnn_setup()
    _L0_gnn_in = {k: v for k, v in _L0_gnn_all.items() if k in ('Wv', 'bv', 'aw', 'ab', 'Wk', 'bk')}
    del _L0_gnn_all

    def _L1_gnn_setup():
        import jax, jax.numpy as jnp
        import numpy as np
        IN_DIM = 256
        ATT_DIM = 64
        B, N = (4, 2048)
        key = jax.random.key(seed)
        k1, k2, k3, k4 = jax.random.split(key, 4)
        x = jax.random.normal(k1, (B, N, IN_DIM), dtype=jnp.float32)
        adj_matrix = (jax.random.uniform(k2, (B, N, N)) < 0.05).astype(jnp.float32)
        W_qk = jax.random.normal(k3, (2 * ATT_DIM, IN_DIM), dtype=jnp.float32) / np.sqrt(IN_DIM)
        W_v = jax.random.normal(k4, (IN_DIM, IN_DIM), dtype=jnp.float32) / np.sqrt(IN_DIM)
        return {'x': x, 'adj_matrix': adj_matrix, 'W_qk': W_qk, 'W_v': W_v}
    _L1_gnn_all = _L1_gnn_setup()
    _L1_gnn_in = {k: v for k, v in _L1_gnn_all.items() if k in ('W_qk', 'W_v')}
    del _L1_gnn_all
    return {'x': x, 'adj': adj, 'L0_gnn_Wv': _L0_gnn_in['Wv'], 'L0_gnn_bv': _L0_gnn_in['bv'], 'L0_gnn_aw': _L0_gnn_in['aw'], 'L0_gnn_ab': _L0_gnn_in['ab'], 'L0_gnn_Wk': _L0_gnn_in['Wk'], 'L0_gnn_bk': _L0_gnn_in['bk'], 'L1_gnn_W_qk': _L1_gnn_in['W_qk'], 'L1_gnn_W_v': _L1_gnn_in['W_v']}

def reference(x, adj, L0_gnn_Wv, L0_gnn_bv, L0_gnn_aw, L0_gnn_ab, L0_gnn_Wk, L0_gnn_bk, L1_gnn_W_qk, L1_gnn_W_v):
    import jax
    import jax.numpy as jnp

    def _L0_gnn_ref(X, A, Wv, bv, aw, ab, Wk, bk):
        import jax, jax.numpy as jnp
        import numpy as np
        B, N, DIN, DOUT, K = (4, 1024, 256, 256, 3)
        d = Wv.shape[1]
        Xw = X @ Wv + bv
        sj = Xw @ aw[:d, 0]
        si = Xw @ aw[d:, 0]
        e = jax.nn.leaky_relu(sj[:, None, :] + si[:, :, None] + ab[0], negative_slope=0.2)
        alpha_matrix = A * jnp.exp(e)
        transition = alpha_matrix / (jnp.sum(alpha_matrix, axis=-1, keepdims=True) + 1e-12)
        H = jnp.zeros(X.shape[:-1] + (d,), dtype=X.dtype)
        Xk = X
        for k in range(Wk.shape[0]):
            H = H + Xk @ Wk[k] + bk[k]
            Xk = jnp.einsum('bij,bjd->bid', transition, Xk)
        return jax.nn.relu(H)

    def _L1_gnn_ref(x, adj_matrix, W_qk, W_v):
        import jax, jax.numpy as jnp
        import numpy as np
        IN_DIM = 256
        ATT_DIM = 64
        B, N = (4, 2048)
        qk = jnp.einsum('bnd,ed->bne', x, W_qk)
        q, k = jnp.split(qk, 2, axis=-1)
        v = jnp.einsum('bnd,ed->bne', x, W_v)
        inv_scale = 1.0 / ATT_DIM ** 0.5
        scores = jnp.einsum('bnd,bmd->bnm', q, k) * inv_scale
        w = jnp.sum(scores * adj_matrix, axis=-1, keepdims=True)
        w = jax.nn.softmax(w, axis=1)
        return w * v
    x = _layernorm(x + _L0_gnn_ref(x, adj, L0_gnn_Wv, L0_gnn_bv, L0_gnn_aw, L0_gnn_ab, L0_gnn_Wk, L0_gnn_bk), axis=-1)
    x = _layernorm(x + _L1_gnn_ref(x, adj, L1_gnn_W_qk, L1_gnn_W_v), axis=-1)
    return x

_drawn_inputs = setup_inputs


def setup_inputs(seed=0):
    import zlib

    import numpy as np

    out = dict(_drawn_inputs(seed))
    spreads = {}
    factors = {'L0_gnn_Wv': 6.38,
     'L0_gnn_bv': 31.459,
     'L0_gnn_aw': 6.566,
     'L1_gnn_W_qk': 4.938,
     'L1_gnn_W_v': 5.017}
    for name, (base, spread) in spreads.items():
        noise = np.random.default_rng([zlib.crc32(name.encode()), seed]).standard_normal(out[name].shape)
        drawn = base * np.exp(spread * noise) if base else spread * noise
        out[name] = jnp.asarray(drawn.astype(out[name].dtype))
    for name, factor in factors.items():
        out[name] = (out[name] * factor).astype(out[name].dtype)
    return out
```

```python
from contextlib import ExitStack

import concourse.bass as bass
from concourse import mybir

P = 128
F32 = mybir.dt.float32
F32R = mybir.dt.float32r
ALU = mybir.AluOpType
ACT = mybir.ActivationFunctionType
AX_X = mybir.AxisListType.X

EPS = 1e-5
ROW_EPS = 1e-12
SLOPE = 0.2


def bass_gnn_pair(nc, xT, x, adjT, Wv, bv, aw, ab, Wk, bk, WqkT, WvT, out):
    B, N, D = x.shape
    NT = N // P
    DC = D // P
    HALF = N // 2
    NH = N // HALF
    TPH = NT // NH
    E = WqkT.shape[1] // 2
    SCALE = 1.0 / float(E) ** 0.5
    K = Wk.shape[0]
    UNITS = NH * NT
    XC = 4
    XCW = N // XC
    XS, AS, GS, SS = 2, 4, 4, 4
    ADMAS = UNITS // 2
    assert K == 3 and D == 2 * P and HALF == 512 and 2 * E == P

    with ExitStack() as ctx:
        def sb(name, shape, dt=F32):
            return ctx.enter_context(nc.sbuf_tensor(name, shape, dt))

        def psum(name, shape):
            return ctx.enter_context(nc.psum_tensor(name, shape, F32))

        def sem(name):
            return ctx.enter_context(nc.semaphore(name))

        a_hi = sb("a_hi", [P, NT, N], F32R)
        a_lo = sb("a_lo", [P, NT, N], F32R)
        adj_a = sb("adj_a", [P, AS, 2, HALF])
        adj_g = sb("adj_g", [P, GS, N])
        unit = sb("unit", [P, SS, HALF])
        row_acc = sb("row_acc", [P, N])
        xt_raw = sb("xt_raw", [P, XS, DC, XCW])
        xt_hi = sb("xt_hi", [P, DC, N], F32R)
        xt_lo = sb("xt_lo", [P, DC, N], F32R)
        y_cat = sb("y_cat", [P, NT, 2 * D], F32R)
        z_cat = sb("z_cat", [P, NT, 2 * D], F32R)
        xw = sb("xw", [P, NT, 2 * D])
        xn = sb("xn", [P, NT, D])
        qk = sb("qk", [P, NT, 2 * E])
        w2_hi, w2_lo = (sb(f"w2_{h}", [P, DC, D + 2], F32R) for h in ("hi", "lo"))
        w10_hi, w10_lo = (sb(f"w10_{h}", [P, DC, 2 * D], F32R) for h in ("hi", "lo"))
        wqk_hi, wqk_lo = (sb(f"wqk_{h}", [P, DC, 2 * E], F32R) for h in ("hi", "lo"))
        wv_hi, wv_lo = (sb(f"wv_{h}", [P, DC, D], F32R) for h in ("hi", "lo"))
        ui_hi, ui_lo = (sb(f"ui_{h}", [P, DC, P], F32R) for h in ("hi", "lo"))
        bias_row = sb("bias_row", [P, 2 * D])
        ident = sb("ident", [P, P])
        ones = sb("ones", [P, P])
        neg_half = sb("neg_half", [P, TPH])
        u_cols = sb("u_cols", [P, 2, DC])
        c_parts = sb("c_parts", [P, 3])
        c_col = sb("c_col", [P, 1])
        ab_col = sb("ab_col", [P, 1])
        sj_rest = sb("sj_rest", [P, NT])
        sj_slope = sb("sj_slope", [P, NT])
        si_slope = sb("si_slope", [P, N])
        rinv = sb("rinv", [P, NT])
        stats = sb("stats", [P, NT, 6])
        mv = sb("mv", [P, NT, 2])
        var_e = sb("var_e", [P, NT])
        rstd = sb("rstd", [P, NT])
        w_col = sb("w_col", [P, NT])
        w_max = sb("w_max", [P, 1])
        g_max = sb("g_max", [1, 1])
        n_max = sb("n_max", [P, 1])
        e_col = sb("e_col", [P, NT])
        e_sum = sb("e_sum", [P, 1])
        t_inv = sb("t_inv", [P, 1])
        p_col = sb("p_col", [P, NT])
        qg = sb("qg", [P, NT, E])

        x1t_hi = z_cat[:, 0:NT // 2, :].rearrange("p a b -> p (a b)").rearrange("p (c n) -> p c n", c=DC)
        x1t_lo = z_cat[:, NT // 2:NT, :].rearrange("p a b -> p (a b)").rearrange("p (c n) -> p c n", c=DC)

        hop = [psum(f"hop{i}", [P, 512]) for i in range(2)]
        si_b = [psum(f"si_b{i}", [P, HALF]) for i in range(NH)]
        gen = [psum(f"gen{i}", [P, 512]) for i in range(3)]
        misc = psum("misc", [P, 512])
        p_rows = misc[:, 0:NT]
        p_maxT = misc[0:1, 64:64 + P]
        p_maxB = misc[:, 256:257]
        p_tot = misc[:, 320:321]

        s_par = sem("s_par")
        s_xt = [sem(f"s_xt{i}") for i in range(XS)]
        s_adja = [sem(f"s_adja{i}") for i in range(AS)]
        s_adjg = [sem(f"s_adjg{i}") for i in range(GS)]
        s_xn = sem("s_xn")
        s_out = sem("s_out")
        s_const = sem("s_const")
        s_id0 = sem("s_id0")
        s_set = sem("s_set")
        s_setv = sem("s_setv")
        s_whi = sem("s_whi")
        s_wready = sem("s_wready")
        si_done = sem("si_done")
        xw2_done = sem("xw2_done")
        hop_done = sem("hop_done")
        xw10_done = sem("xw10_done")
        x1t_done = sem("x1t_done")
        qk_done = sem("qk_done")
        g_done = sem("g_done")
        rows_done = sem("rows_done")
        maxT_done = sem("maxT_done")
        maxB_done = sem("maxB_done")
        tot_done = sem("tot_done")
        v_done = sem("v_done")
        xt_hi_done = sem("xt_hi_done")
        z_hi_done = sem("z_hi_done")
        y_hi_done = sem("y_hi_done")
        si_slope_done = sem("si_slope_done")
        exp_done = sem("exp_done")
        a_hi_done = sem("a_hi_done")
        x1t_hi_done = sem("x1t_hi_done")
        qk_copied = sem("qk_copied")
        p_exp_done = sem("p_exp_done")
        xt_lo_done = sem("xt_lo_done")
        rinv_done = sem("rinv_done")
        rsum_done = sem("rsum_done")
        hop1_part = sem("hop1_part")
        z_done = sem("z_done")
        y_lo_done = sem("y_lo_done")
        hop2_part = sem("hop2_part")
        h_done = sem("h_done")
        res_done = sem("res_done")
        stats_done = sem("stats_done")
        aggr_done = sem("aggr_done")
        var_done = sem("var_done")
        x1_done = sem("x1_done")
        lrelu_done = sem("lrelu_done")
        alpha_done = sem("alpha_done")
        rows_added = sem("rows_added")
        xw10_copied = sem("xw10_copied")
        x1t_lo_done = sem("x1t_lo_done")
        qg_done = sem("qg_done")
        w_done = sem("w_done")
        wmax_done = sem("wmax_done")
        gmax_done = sem("gmax_done")
        nmax_done = sem("nmax_done")
        tinv_done = sem("tinv_done")
        p_done = sem("p_done")
        y2_done = sem("y2_done")
        stats2_done = sem("stats2_done")
        aggr2_done = sem("aggr2_done")
        var2_done = sem("var2_done")
        out_done = sem("out_done")
        z_lo_done = sem("z_lo_done")
        a_lo_done = sem("a_lo_done")
        rstd_done = sem("rstd_done")
        rstd2_done = sem("rstd2_done")

        def nth(batch, per_batch, c):
            return batch * per_batch + c

        def has_prior(batch):
            return not isinstance(batch, int) or batch > 0

        U_XW2, U_XW10A, U_X1T, U_QK, U_G, U_XW10B, U_V, USES = 0, 8, 12, 16, 18, 19, 23, 27
        assert USES % 3 == 0

        def bank(idx):
            return gen[idx % 3]

        block = ctx.enter_context(nc.Block())

        def run_slots(eng, slot):
            slot(0, True, False)
            slot(1, True, True)
            with eng.Fori(2, B) as s:
                slot(s, True, True)
            slot(B, False, True)

        w_stage = xw[:, :, :].rearrange("p a b -> p (a b)")
        o = 0
        st = {}
        for nm, wd in (("w2", D), ("w10", 2 * D), ("wqk", 2 * E), ("wv", D)):
            st[nm] = w_stage[:, o:o + DC * wd].rearrange("p (c n) -> p c n", c=DC)
            o += DC * wd
        x_stage = xn[:, :, :].rearrange("p a b -> p (a b)")
        wvn = x_stage[:, 0:DC * D].rearrange("p (c n) -> p c n", c=DC)
        aw_row = x_stage[:, 512:1024]
        bv_row = x_stage[:, 1024:1280]
        bk_rows = x_stage[:, 1280:2048].rearrange("p (k n) -> p k n", k=K)

        @block.sync
        def _(sp):
            def load_xt(f, c):
                if c >= XS:
                    sp.wait_ge(xt_lo_done, nth(f, XC, c - XS + 1))
                else:
                    if has_prior(f):
                        sp.wait_ge(xt_lo_done, nth(f - 1, XC, XC + c - XS + 1))
                sp.dma_start(xt_raw[:, c % XS, :, :],
                             xT[f].rearrange("(c p) n -> p c n", p=P)[:, :, c * XCW:(c + 1) * XCW])\
                    .then_inc(s_xt[c % XS], 16)

            def load_adj_a(f, n):
                if n >= AS:
                    sp.wait_ge(alpha_done, nth(f, UNITS, 2 * (n - AS) + 2))
                else:
                    if has_prior(f):
                        sp.wait_ge(alpha_done, nth(f - 1, UNITS, 2 * (n + ADMAS - AS) + 2))
                h, jt = 2 * n // NT, 2 * n % NT
                sp.dma_start(adj_a[:, n % AS, :, :],
                             adjT[f].rearrange("(j p) i -> p j i", p=P)[:, jt:jt + 2, h * HALF:(h + 1) * HALF])\
                    .then_inc(s_adja[n % AS], 16)

            def load_adj_g(g, mt):
                if mt >= GS:
                    sp.wait_ge(g_done, nth(g, NT, mt - GS + 1))
                else:
                    if has_prior(g):
                        sp.wait_ge(g_done, nth(g - 1, NT, NT + mt - GS + 1))
                sp.dma_start(adj_g[:, mt % GS, :], adjT[g].rearrange("(j p) i -> p j i", p=P)[:, mt, :])\
                    .then_inc(s_adjg[mt % GS], 16)

            def store(g):
                for h in range(2):
                    sp.wait_ge(out_done, nth(g, NT, (h + 1) * NT // 2))
                    sp.dma_start(out[g].rearrange("(t p) d -> p t d", p=P)[:, h * 4:h * 4 + 4, :],
                                 xn[:, h * 4:h * 4 + 4, :]).then_inc(s_out, 16)

            for t, src in ((st["w2"], Wk[2]), (st["w10"][:, :, 0:D], Wk[1]), (st["w10"][:, :, D:2 * D], Wk[0]),
                           (st["wqk"], WqkT), (st["wv"], WvT), (wvn, Wv)):
                sp.dma_start(t, src.rearrange("(c p) n -> p c n", p=P)).then_inc(s_par, 16)
            sp.dma_start(aw_row, aw.rearrange("a o -> o a").to_broadcast([P, 2 * D])).then_inc(s_par, 16)
            sp.dma_start(bv_row, bv.rearrange("(o a) -> o a", o=1).to_broadcast([P, D])).then_inc(s_par, 16)
            for k in range(K):
                sp.dma_start(bk_rows[:, k, :], bk[k:k + 1, :].to_broadcast([P, D])).then_inc(s_par, 16)
            sp.dma_start(ab_col[:, :], ab.rearrange("(o a) -> o a", o=1).to_broadcast([P, 1])).then_inc(s_par, 16)

            def slot(s, front, back):
                f, g = s, s - 1
                if front:
                    for c in range(XC):
                        load_xt(f, c)
                    for n in range(AS):
                        load_adj_a(f, n)
                if back:
                    for mt in range(GS):
                        load_adj_g(g, mt)
                    if not (isinstance(s, int) and s == 1):
                        store(g - 1)
                        sp.wait_ge(s_out, g * 32)
                    else:
                        sp.wait_ge(s_set, 1)
                    sp.dma_start(xn[:, :, :], x[g].rearrange("(t p) d -> p t d", p=P)).then_inc(s_xn, 16)
                if front:
                    for n in range(AS, ADMAS):
                        load_adj_a(f, n)
                if back:
                    for mt in range(GS, NT):
                        load_adj_g(g, mt)

            run_slots(sp, slot)
            store(B - 1)
            sp.wait_ge(s_out, B * 32)

        @block.gpsimd
        def _(pool):
            nc.gpsimd.memset(ident[:, :], 0.0).then_inc(s_id0, 1)
            pool.wait_ge(s_id0, 1)
            nc.gpsimd.affine_select(out=ident[:, :], in_=ident[:, :], compare_op=ALU.not_equal, fill=1.0,
                                    base=0, pattern=[[-1, P]], channel_multiplier=1).then_inc(s_const, 1)
            nc.gpsimd.memset(neg_half[:, :], -0.5).then_inc(s_const, 1)

            def a_lo_unit(f, g, back, u):
                h, jt = divmod(u, NT)
                if back and jt == 0:
                    pool.wait_ge(hop_done, nth(g, 2 * NT, NT + TPH * (h + 1)))
                pool.wait_ge(a_hi_done, nth(f, UNITS, u + 1))
                cols = slice(h * HALF, (h + 1) * HALF)
                nc.gpsimd.tensor_tensor(a_lo[:, jt, cols], unit[:, u % SS, :], a_hi[:, jt, cols].bitcast(F32),
                                        ALU.subtract).then_inc(a_lo_done, 1)

            def slot(s, front, back):
                f, g = s, s - 1
                if back:
                    for it in range(NT):
                        pool.wait_ge(z_hi_done, nth(g, NT, it + 1))
                        nc.gpsimd.tensor_tensor(z_cat[:, it, D:2 * D], xw[:, it, 0:D],
                                                z_cat[:, it, 0:D].bitcast(F32), ALU.subtract)\
                            .then_inc(z_lo_done, 1)
                if front:
                    for u in range(4):
                        a_lo_unit(f, g, back, u)
                if back:
                    for h in range(2):
                        pool.wait_ge(var_done, nth(g, 2, h + 1))
                        nc.gpsimd.tensor_tensor(rstd[:, 4 * h:4 * h + 4], var_e[:, 4 * h:4 * h + 4],
                                                neg_half[:, 0:4], ALU.pow).then_inc(rstd_done, 1)
                if front:
                    for u in range(4, UNITS):
                        a_lo_unit(f, g, back, u)
                if back:
                    for h in range(2):
                        pool.wait_ge(var2_done, nth(g, 2, h + 1))
                        nc.gpsimd.tensor_tensor(rstd[:, 4 * h:4 * h + 4], var_e[:, 4 * h:4 * h + 4],
                                                neg_half[:, 0:4], ALU.pow).then_inc(rstd2_done, 1)

            run_slots(pool, slot)

        @block.scalar
        def _(act):
            act.wait_ge(s_par, 12 * 16)
            nc.scalar.copy(w2_hi[:, :, 0:D], st["w2"])
            nc.scalar.copy(w10_hi[:, :, :], st["w10"])
            nc.scalar.copy(wqk_hi[:, :, :], st["wqk"])
            nc.scalar.copy(wv_hi[:, :, :], st["wv"]).then_inc(s_whi, 1)

            def exp_unit(f, u):
                act.wait_ge(lrelu_done, nth(f, UNITS, u + 1))
                jt = u % NT
                nc.scalar.activation(unit[:, u % SS, :], unit[:, u % SS, :], ACT.Exp, bias=sj_slope[:, jt:jt + 1])\
                    .then_inc(exp_done, 1)

            def a_hi_unit(f, g, back, u):
                h, jt = divmod(u, NT)
                if back and jt == 0:
                    act.wait_ge(hop_done, nth(g, 2 * NT, NT + TPH * (h + 1)))
                act.wait_ge(alpha_done, nth(f, UNITS, u + 1))
                nc.scalar.copy(a_hi[:, jt, h * HALF:(h + 1) * HALF], unit[:, u % SS, :]).then_inc(a_hi_done, 1)

            def alpha_step(f, g, back, u):
                if u < UNITS:
                    exp_unit(f, u)
                if u > 0:
                    a_hi_unit(f, g, back, u - 1)

            def x1t_hi_copy(g, i):
                act.wait_ge(x1t_done, nth(g, 4, i + 1))
                if i == 0:
                    act.wait_ge(hop_done, nth(g, 2 * NT, 2 * NT))
                nc.scalar.copy(x1t_hi[:, :, 256 * i:256 * i + 256],
                               bank(U_X1T + i)[:, :].rearrange("p (c n) -> p c n", c=DC))\
                    .then_inc(x1t_hi_done, 1)

            def slot(s, front, back):
                f, g = s, s - 1
                if front:
                    for c in range(XC):
                        act.wait_ge(s_xt[c % XS], f * 16 * (XC // XS) + 16 * (c // XS + 1))
                        if c == 0:
                            if has_prior(f):
                                act.wait_ge(xw10_done, nth(f - 1, NT, NT))
                        nc.scalar.copy(xt_hi[:, :, c * XCW:(c + 1) * XCW], xt_raw[:, c % XS, :, :])\
                            .then_inc(xt_hi_done, 1)
                if back:
                    if has_prior(g):
                        act.wait_ge(v_done, nth(g - 1, 4, 4))
                    for it in range(NT):
                        act.wait_ge(z_done, nth(g, NT, it + 1))
                        nc.scalar.copy(z_cat[:, it, 0:D], xw[:, it, 0:D]).then_inc(z_hi_done, 1)
                if front:
                    for nt in range(NT):
                        act.wait_ge(xw2_done, nth(f, NT, nt + 1))
                        nc.scalar.copy(y_cat[:, nt, 0:D], bank(U_XW2 + nt)[:, 0:D]).then_inc(y_hi_done, 1)
                    for h in range(NH):
                        act.wait_ge(si_done, nth(f, NH, h + 1))
                        if h == 0:
                            if has_prior(f):
                                act.wait_ge(lrelu_done, nth(f - 1, UNITS, UNITS))
                        nc.scalar.mul(si_slope[:, h * HALF:(h + 1) * HALF], si_b[h][:, :], SLOPE)\
                            .then_inc(si_slope_done, 1)
                    for u in range(8):
                        alpha_step(f, g, back, u)
                for i in range(4):
                    if back:
                        x1t_hi_copy(g, i)
                    if front:
                        alpha_step(f, g, back, 8 + i)
                for i in range(2):
                    if back:
                        act.wait_ge(qk_done, nth(g, 2, i + 1))
                        nc.scalar.copy(qk[:, 4 * i:4 * i + 4, :],
                                       bank(U_QK + i)[:, :].rearrange("p (t e) -> p t e", t=4))\
                            .then_inc(qk_copied, 1)
                    if front:
                        alpha_step(f, g, back, 12 + 2 * i)
                        alpha_step(f, g, back, 13 + 2 * i)
                if front:
                    alpha_step(f, g, back, UNITS)
                if back:
                    act.wait_ge(nmax_done, nth(g, 1, 1))
                    nc.scalar.activation(e_col[:, :], w_col[:, :], ACT.Exp, bias=n_max[:, :], scale=SCALE,
                                         accum_out=e_sum[:, :]).then_inc(p_exp_done, 1)

            run_slots(act, slot)

        @block.vector
        def _(dve):
            V = nc.vector
            n_set = [0]

            def step(ins):
                n_set[0] += 1
                ins.then_inc(s_setv, 1)
                dve.wait_ge(s_setv, n_set[0])

            step(V.memset(ones[:, :], 1.0))
            step(V.memset(bias_row[:, 0:D], 0.0))
            dve.wait_ge(s_par, 12 * 16)
            prod = qg[:, :, :].rearrange("p a b -> p (a b)")[:, 0:D]
            for a in range(2):
                for c in range(DC):
                    step(V.tensor_tensor(prod, wvn[:, c, :], aw_row[:, a * D:(a + 1) * D], ALU.mult))
                    step(V.tensor_reduce(u_cols[:, a, c:c + 1], prod, AX_X, ALU.add))
                step(V.tensor_tensor(prod, bv_row, aw_row[:, a * D:(a + 1) * D], ALU.mult))
                step(V.tensor_reduce(c_parts[:, a:a + 1], prod, AX_X, ALU.add))
            step(V.tensor_copy(c_parts[:, 2:3], ab_col[:, :]))
            step(V.tensor_reduce(c_col[:, :], c_parts[:, :], AX_X, ALU.add))
            step(V.tensor_tensor(prod, bk_rows[:, 0, :], bk_rows[:, 1, :], ALU.add))
            step(V.tensor_tensor(bias_row[:, D:2 * D], prod, bk_rows[:, 2, :], ALU.add))
            for c in range(DC):
                step(V.tensor_copy(w2_hi[:, c, D:D + 2], u_cols[:, 0, c:c + 1].to_broadcast([P, 2])))
                step(V.tensor_tensor(w2_lo[:, c, D:D + 2], u_cols[:, 0, c:c + 1].to_broadcast([P, 2]),
                                     w2_hi[:, c, D:D + 2].bitcast(F32), ALU.subtract))
                ub = prod[:, 0:P]
                step(V.tensor_scalar(ub, ones[:, :], u_cols[:, 1, c:c + 1], None, ALU.mult))
                step(V.tensor_copy(ui_hi[:, c, :], ub))
                step(V.tensor_tensor(ui_lo[:, c, :], ub, ui_hi[:, c, :].bitcast(F32), ALU.subtract))
            dve.wait_ge(s_whi, 1)
            for raw, hi, lo in ((st["w2"], w2_hi[:, :, 0:D], w2_lo[:, :, 0:D]), (st["w10"], w10_hi[:, :, :], w10_lo[:, :, :]),
                                (st["wqk"], wqk_hi[:, :, :], wqk_lo[:, :, :]), (st["wv"], wv_hi[:, :, :], wv_lo[:, :, :])):
                last = V.tensor_tensor(lo, raw, hi.bitcast(F32), ALU.subtract)
            last.then_inc(s_set, 1)
            dve.wait_ge(s_set, 1)

            def lrelu_unit(f, u):
                h, jt = divmod(u, NT)
                if u >= SS:
                    dve.wait_ge(a_hi_done, nth(f, UNITS, u - SS + 1))
                    dve.wait_ge(a_lo_done, nth(f, UNITS, u - SS + 1))
                    dve.wait_ge(rows_added, nth(f, UNITS, u - SS + 1))
                elif has_prior(f):
                    dve.wait_ge(a_hi_done, nth(f - 1, UNITS, UNITS + u - SS + 1))
                    dve.wait_ge(a_lo_done, nth(f - 1, UNITS, UNITS + u - SS + 1))
                    dve.wait_ge(rows_added, nth(f - 1, UNITS, UNITS + u - SS + 1))
                if u == 0:
                    dve.wait_ge(y_lo_done, nth(f, NT, NT))
                if jt == 0:
                    dve.wait_ge(si_slope_done, nth(f, NH, h + 1))
                V.scalar_tensor_tensor(unit[:, u % SS, :], si_b[h][:, :], sj_rest[:, jt:jt + 1],
                                       si_slope[:, h * HALF:(h + 1) * HALF], ALU.add, ALU.max)\
                    .then_inc(lrelu_done, 1)

            def alpha_unit(f, u):
                if u == 0:
                    lrelu_unit(f, 0)
                    lrelu_unit(f, 1)
                if u + 2 < UNITS:
                    lrelu_unit(f, u + 2)
                h, jt = divmod(u, NT)
                n = u // 2
                cols = slice(h * HALF, (h + 1) * HALF)
                dve.wait_ge(exp_done, nth(f, UNITS, u + 1))
                dve.wait_ge(s_adja[n % AS], f * 16 * (ADMAS // AS) + 16 * (n // AS + 1))
                V.tensor_tensor(unit[:, u % SS, :], unit[:, u % SS, :], adj_a[:, n % AS, u % 2, :], ALU.mult)\
                    .then_inc(alpha_done, 1)
                dve.wait_ge(alpha_done, nth(f, UNITS, u + 1))
                if jt == 0:
                    if u == 0:
                        if has_prior(f):
                            dve.wait_ge(rows_done, nth(f - 1, NH, NH))
                    V.tensor_copy(row_acc[:, cols], unit[:, u % SS, :]).then_inc(rows_added, 1)
                else:
                    dve.wait_ge(rows_added, nth(f, UNITS, u))
                    V.tensor_tensor(row_acc[:, cols], row_acc[:, cols], unit[:, u % SS, :], ALU.add)\
                        .then_inc(rows_added, 1)

            def rows_inverse(g, h):
                dve.wait_ge(rows_done, nth(g, NH, h + 1))
                cols = slice(TPH * h, TPH * h + TPH)
                V.tensor_scalar(rinv[:, cols], p_rows[:, cols], ROW_EPS, None, ALU.add).then_inc(rsum_done, 1)
                dve.wait_ge(rsum_done, nth(g, NH, h + 1))
                V.reciprocal(rinv[:, cols], rinv[:, cols]).then_inc(rinv_done, 1)

            def xw10_copy(f, nt):
                dve.wait_ge(xw10_done, nth(f, NT, nt + 1))
                idx = U_XW10A + nt if nt < 4 else U_XW10B + nt - 4
                V.tensor_tensor(xw[:, nt, :], bank(idx)[:, :], bias_row[:, :], ALU.add).then_inc(xw10_copied, 1)

            def norm(g, h, aggr, var):
                V.memset(var_e[:, 4 * h:4 * h + 4], EPS)
                for t in range(4 * h, 4 * h + 4):
                    V.bn_aggr(mv[:, t, :], stats[:, t, :]).then_inc(aggr, 1)
                dve.wait_ge(aggr, nth(g, NT, 4 * h + 4))
                V.tensor_tensor(var_e[:, 4 * h:4 * h + 4], mv[:, 4 * h:4 * h + 4, 1], var_e[:, 4 * h:4 * h + 4],
                                ALU.add)\
                    .then_inc(var, 1)

            def normalise(g, h, rstd_sem, done):
                dve.wait_ge(rstd_sem, nth(g, 2, h + 1))
                for t in range(4 * h, 4 * h + 4):
                    V.tensor_scalar(xn[:, t, :], xn[:, t, :], mv[:, t, 0:1], rstd[:, t:t + 1],
                                    ALU.subtract, ALU.mult).then_inc(done, 1)

            def slot(s, front, back):
                f, g = s, s - 1
                if front:
                    for c in range(XC):
                        dve.wait_ge(xt_hi_done, nth(f, XC, c + 1))
                        V.tensor_tensor(xt_lo[:, :, c * XCW:(c + 1) * XCW], xt_raw[:, c % XS, :, :],
                                        xt_hi[:, :, c * XCW:(c + 1) * XCW].bitcast(F32), ALU.subtract)\
                            .then_inc(xt_lo_done, 1)
                if back:
                    for it in range(NT):
                        if it % TPH == 0:
                            rows_inverse(g, it // TPH)
                        dve.wait_ge(hop_done, nth(g, 2 * NT, it + 1))
                        if it % TPH == 0:
                            dve.wait_ge(rinv_done, nth(g, NH, it // TPH + 1))
                        V.scalar_tensor_tensor(xw[:, it, 0:D], hop[it % 2][:, D:2 * D], rinv[:, it:it + 1],
                                               xw[:, it, 0:D], ALU.mult, ALU.add).then_inc(hop1_part, 1)
                        dve.wait_ge(hop1_part, nth(g, NT, it + 1))
                        V.scalar_tensor_tensor(xw[:, it, 0:D], hop[it % 2][:, 0:D], rinv[:, it:it + 1],
                                               xw[:, it, 0:D], ALU.mult, ALU.add).then_inc(z_done, 1)
                if front:
                    for nt in range(NT):
                        dve.wait_ge(y_hi_done, nth(f, NT, nt + 1))
                        sj_raw = bank(U_XW2 + nt)[:, D:D + 1]
                        V.tensor_scalar(sj_rest[:, nt:nt + 1], sj_raw, c_col[:, :], 1.0 - SLOPE, ALU.add, ALU.mult)
                        V.tensor_scalar(sj_slope[:, nt:nt + 1], sj_raw, c_col[:, :], SLOPE, ALU.add, ALU.mult)
                        V.tensor_tensor(y_cat[:, nt, D:2 * D], bank(U_XW2 + nt)[:, 0:D],
                                        y_cat[:, nt, 0:D].bitcast(F32), ALU.subtract).then_inc(y_lo_done, 1)
                if back:
                    s_x = 16 * (g + 1)
                    for it in range(NT):
                        dve.wait_ge(hop_done, nth(g, 2 * NT, NT + it + 1))
                        if it == 0:
                            dve.wait_ge(s_xn, s_x)
                        V.scalar_tensor_tensor(xw[:, it, D:2 * D], hop[it % 2][:, D:2 * D], rinv[:, it:it + 1],
                                               xw[:, it, D:2 * D], ALU.mult, ALU.add).then_inc(hop2_part, 1)
                        dve.wait_ge(hop2_part, nth(g, NT, it + 1))
                        V.scalar_tensor_tensor(xw[:, it, D:2 * D], hop[it % 2][:, 0:D], rinv[:, it:it + 1],
                                               xw[:, it, D:2 * D], ALU.mult, ALU.add).then_inc(h_done, 1)
                        dve.wait_ge(h_done, nth(g, NT, it + 1))
                        V.scalar_tensor_tensor(xn[:, it, :], xw[:, it, D:2 * D], 0.0, xn[:, it, :],
                                               ALU.max, ALU.add).then_inc(res_done, 1)
                        dve.wait_ge(res_done, nth(g, NT, it + 1))
                        V.bn_stats(stats[:, it, :], xn[:, it, :]).then_inc(stats_done, 1)
                        if front and it >= 4:
                            alpha_unit(f, it - 4)
                        if it == 4:
                            dve.wait_ge(stats_done, nth(g, NT, 4))
                            norm(g, 0, aggr_done, var_done)
                    dve.wait_ge(stats_done, nth(g, NT, NT))
                    norm(g, 1, aggr_done, var_done)
                    normalise(g, 0, rstd_done, x1_done)
                    normalise(g, 1, rstd_done, x1_done)
                if front:
                    for i in range(4):
                        xw10_copy(f, i)
                        if not back:
                            alpha_unit(f, i)
                    for u in range(4, 8):
                        alpha_unit(f, u)
                for i in range(4):
                    if back:
                        dve.wait_ge(x1t_hi_done, nth(g, 4, i + 1))
                        V.tensor_tensor(x1t_lo[:, :, 256 * i:256 * i + 256],
                                        bank(U_X1T + i)[:, :].rearrange("p (c n) -> p c n", c=DC),
                                        x1t_hi[:, :, 256 * i:256 * i + 256].bitcast(F32), ALU.subtract)\
                            .then_inc(x1t_lo_done, 1)
                    if front:
                        alpha_unit(f, 8 + i)
                if front:
                    alpha_unit(f, 12)
                    alpha_unit(f, 13)
                if back:
                    dve.wait_ge(g_done, nth(g, NT, NT))
                    V.tensor_tensor(qg[:, :, :], bank(U_G)[:, :].rearrange("p (t e) -> p t e", t=NT), qk[:, :, 0:E],
                                    ALU.mult).then_inc(qg_done, 1)
                    dve.wait_ge(qg_done, nth(g, 1, 1))
                    V.tensor_reduce(w_col[:, :], qg[:, :, :], AX_X, ALU.add).then_inc(w_done, 1)
                    dve.wait_ge(w_done, nth(g, 1, 1))
                    V.tensor_reduce(w_max[:, :], w_col[:, :], AX_X, ALU.max).then_inc(wmax_done, 1)
                if front:
                    xw10_copy(f, 4)
                if back:
                    dve.wait_ge(maxT_done, nth(g, 1, 1))
                    V.tensor_reduce(g_max[:, :], p_maxT, AX_X, ALU.max).then_inc(gmax_done, 1)
                if front:
                    xw10_copy(f, 5)
                if back:
                    dve.wait_ge(maxB_done, nth(g, 1, 1))
                    V.tensor_scalar(n_max[:, :], p_maxB, -SCALE, None, ALU.mult).then_inc(nmax_done, 1)
                if front:
                    xw10_copy(f, 6)
                    xw10_copy(f, 7)
                    alpha_unit(f, 14)
                    alpha_unit(f, 15)
                if back:
                    dve.wait_ge(tot_done, nth(g, 1, 1))
                    V.reciprocal(t_inv[:, :], p_tot).then_inc(tinv_done, 1)
                    dve.wait_ge(tinv_done, nth(g, 1, 1))
                    V.tensor_scalar(p_col[:, :], e_col[:, :], t_inv[:, :], None, ALU.mult).then_inc(p_done, 1)
                    dve.wait_ge(p_done, nth(g, 1, 1))
                    for it in range(NT):
                        dve.wait_ge(v_done, nth(g, 4, it // 2 + 1))
                        V.scalar_tensor_tensor(xn[:, it, :], bank(U_V + it // 2)[:, (it % 2) * D:(it % 2 + 1) * D],
                                               p_col[:, it:it + 1], xn[:, it, :], ALU.mult, ALU.add)\
                            .then_inc(y2_done, 1)
                        dve.wait_ge(y2_done, nth(g, NT, it + 1))
                        V.bn_stats(stats[:, it, :], xn[:, it, :]).then_inc(stats2_done, 1)
                        if it % 4 == 3:
                            dve.wait_ge(stats2_done, nth(g, NT, it + 1))
                            norm(g, it // 4, aggr2_done, var2_done)
                    normalise(g, 0, rstd2_done, out_done)
                    normalise(g, 1, rstd2_done, out_done)

            run_slots(dve, slot)

        @block.tensor
        def _(pe):
            mm = nc.tensor.matmul

            def mm3(o, l_hi, l_lo, r_hi, r_lo, first, last):
                mm(o, l_hi, r_hi, start=first, stop=False)
                mm(o, l_hi, r_lo, start=False, stop=False)
                return mm(o, l_lo, r_hi, start=False, stop=last)

            pe.wait_ge(s_const, 1)
            pe.wait_ge(s_set, 1)

            def row_sums(g, h):
                pe.wait_ge(rows_added, nth(g, UNITS, NT * (h + 1)))
                if h:
                    pe.wait_ge(rinv_done, nth(g, NH, h))
                else:
                    if has_prior(g):
                        pe.wait_ge(tinv_done, nth(g - 1, 1, 1))
                for it in range(TPH * h, TPH * h + TPH):
                    last = mm(misc[:, it:it + 1], row_acc[:, it * P:(it + 1) * P], ones[:, 0:1], start=True, stop=True)
                last.then_inc(rows_done, 1)

            def hop_tile(g, n, cat, it):
                if n == 0 and it < 2:
                    if has_prior(g):
                        pe.wait_ge(h_done, nth(g - 1, NT, NT + it - 1))
                elif it < 2:
                    pe.wait_ge(z_done, nth(g, NT, NT + it - 1))
                else:
                    pe.wait_ge(h_done if n else z_done, nth(g, NT, it - 1))
                o = hop[it % 2]
                for jt in range(NT):
                    blk = slice(it * P, (it + 1) * P)
                    mm(o[:, :], a_hi[:, jt, blk], cat[:, jt, :], start=(jt == 0), stop=False)
                    last = mm(o[:, 0:D], a_lo[:, jt, blk], cat[:, jt, 0:D], start=False, stop=(jt == NT - 1))
                last.then_inc(hop_done, 1)

            def xw10(f, back, nt):
                idx = U_XW10A + nt if nt < 4 else U_XW10B + nt - 4
                if nt < 3:
                    pe.wait_ge(y_lo_done, nth(f, NT, NT - 2 + nt))
                elif nt == 3:
                    pe.wait_ge(xw10_copied, nth(f, NT, 1))
                elif not back:
                    pe.wait_ge(xw10_copied, nth(f, NT, nt - 1))
                elif nt == 6:
                    pe.wait_ge(qg_done, nth(f - 1, 1, 1))
                elif nt == 7:
                    pe.wait_ge(xw10_copied, nth(f, NT, 5))
                for c in range(DC):
                    last = mm3(bank(idx)[:, :], xt_hi[:, c, nt * P:(nt + 1) * P], xt_lo[:, c, nt * P:(nt + 1) * P],
                               w10_hi[:, c, :], w10_lo[:, c, :], c == 0, c == DC - 1)
                last.then_inc(xw10_done, 1)

            def slot(s, front, back):
                f, g = s, s - 1
                if back:
                    pe.wait_ge(y_lo_done, nth(g, NT, NT))
                    for it in range(NT):
                        if it % TPH == 0:
                            h = it // TPH
                            row_sums(g, h)
                            pe.wait_ge(a_hi_done, nth(g, UNITS, NT * (h + 1)))
                            pe.wait_ge(a_lo_done, nth(g, UNITS, NT * (h + 1)))
                        hop_tile(g, 0, y_cat, it)
                if front:
                    for h in range(NH):
                        pe.wait_ge(xt_lo_done, nth(f, XC, (h + 1) * XC // NH))
                        if h == 0:
                            if has_prior(f):
                                pe.wait_ge(lrelu_done, nth(f - 1, UNITS, UNITS))
                        for c in range(DC):
                            cols = slice(h * HALF, (h + 1) * HALF)
                            last = mm3(si_b[h][:, :], ui_hi[:, c, :], ui_lo[:, c, :], xt_hi[:, c, cols],
                                       xt_lo[:, c, cols], c == 0, c == DC - 1)
                        last.then_inc(si_done, 1)
                    for nt in range(NT):
                        if nt >= 3:
                            pe.wait_ge(y_lo_done, nth(f, NT, nt - 2))
                        elif back and has_prior(g):
                            pe.wait_ge(y2_done, nth(g - 1, NT, 2 * nt + 4))
                        elif back:
                            pe.wait_ge(xw10_copied, nth(f - 1, NT, NT))
                        for c in range(DC):
                            last = mm3(bank(U_XW2 + nt)[:, 0:D + 2], xt_hi[:, c, nt * P:(nt + 1) * P],
                                       xt_lo[:, c, nt * P:(nt + 1) * P], w2_hi[:, c, :], w2_lo[:, c, :],
                                       c == 0, c == DC - 1)
                        last.then_inc(xw2_done, 1)
                if back:
                    pe.wait_ge(z_lo_done, nth(g, NT, NT))
                    for it in range(NT):
                        hop_tile(g, 1, z_cat, it)
                if front:
                    for nt in range(4):
                        if nt == 0 and back:
                            pe.wait_ge(h_done, nth(g, NT, NT))
                        xw10(f, back, nt)
                if back:
                    for i in range(4):
                        pe.wait_ge(x1_done, nth(g, NT, 2 * i + 2))
                        if i == 3:
                            pe.wait_ge(x1t_lo_done, nth(g, 4, 1))
                        elif front:
                            pe.wait_ge(xw10_copied, nth(f, NT, i + 2))
                        else:
                            pe.wait_ge(y2_done, nth(g - 1, NT, 2 * i + 4))
                        b = bank(U_X1T + i)
                        for c in range(DC):
                            for j in range(2):
                                nt = 2 * i + j
                                last = nc.tensor.transpose(b[:, c * 256 + j * P:c * 256 + (j + 1) * P],
                                                           xn[:, nt, c * P:(c + 1) * P], ident[:, :])
                        last.then_inc(x1t_done, 1)
                    for i in range(2):
                        pe.wait_ge(x1t_lo_done, nth(g, 4, 2 * i + 2))
                        for j in range(4):
                            nt = 4 * i + j
                            for c in range(DC):
                                blk = slice(nt * P, (nt + 1) * P)
                                last = mm3(bank(U_QK + i)[:, j * P:(j + 1) * P], x1t_hi[:, c, blk], x1t_lo[:, c, blk],
                                           wqk_hi[:, c, :], wqk_lo[:, c, :], c == 0, c == DC - 1)
                        last.then_inc(qk_done, 1)
                    for mt in range(NT):
                        if mt % 4 == 0:
                            pe.wait_ge(qk_copied, nth(g, 2, mt // 4 + 1))
                        pe.wait_ge(s_adjg[mt % GS], g * 16 * (NT // GS) + 16 * (mt // GS + 1))
                        for it in range(NT):
                            last = mm(bank(U_G)[:, it * E:(it + 1) * E], adj_g[:, mt % GS, it * P:(it + 1) * P],
                                      qk[:, mt, E:2 * E], start=(mt == 0 and it == 0), stop=(mt == NT - 1),
                                      skip_group_check=True)
                        last.then_inc(g_done, 1)
                if front:
                    xw10(f, back, 4)
                    xw10(f, back, 5)
                if back:
                    pe.wait_ge(wmax_done, nth(g, 1, 1))
                    nc.tensor.transpose(p_maxT, w_max[:, :], ident[:, :]).then_inc(maxT_done, 1)
                if front:
                    xw10(f, back, 6)
                if back:
                    pe.wait_ge(gmax_done, nth(g, 1, 1))
                    mm(p_maxB, ones[0:1, :], g_max[:, :], start=True, stop=True).then_inc(maxB_done, 1)
                if front:
                    xw10(f, back, 7)
                if back:
                    for i in range(3):
                        v_tiles(g, front, i)
                    pe.wait_ge(p_exp_done, nth(g, 1, 1))
                    mm(p_tot, ones[:, :], e_sum[:, :], start=True, stop=True).then_inc(tot_done, 1)
                    v_tiles(g, front, 3)

            def v_tiles(g, front, i):
                if i == 3:
                    pe.wait_ge(y2_done, nth(g, NT, 2))
                elif front:
                    pe.wait_ge(xw10_copied, nth(g + 1, NT, 6 + i))
                for j in range(2):
                    blk = slice((2 * i + j) * P, (2 * i + j + 1) * P)
                    for c in range(DC):
                        last = mm3(bank(U_V + i)[:, j * D:(j + 1) * D], x1t_hi[:, c, blk], x1t_lo[:, c, blk],
                                   wv_hi[:, c, :], wv_lo[:, c, :], c == 0, c == DC - 1)
                last.then_inc(v_done, 1)

            run_slots(pe, slot)


def kernel(x, adj, L0_gnn_Wv, L0_gnn_bv, L0_gnn_aw, L0_gnn_ab, L0_gnn_Wk, L0_gnn_bk, L1_gnn_W_qk, L1_gnn_W_v):
    import numpy as np
    import concourse.bacc as bacc
    from concourse import mybir as mb
    from concourse.bass_utils import run_bass_kernel_spmd as run

    nc = bacc.Bacc("TRN2", target_bir_lowering=False, num_devices=1, dynamic_dma_scratch_size=1024)
    laid = {
        "xT": np.asarray(x).transpose(0, 2, 1), "x": x, "adjT": np.asarray(adj).transpose(0, 2, 1),
        "Wv": L0_gnn_Wv, "bv": L0_gnn_bv, "aw": L0_gnn_aw, "ab": L0_gnn_ab, "Wk": L0_gnn_Wk, "bk": L0_gnn_bk,
        "WqkT": np.asarray(L1_gnn_W_qk).T, "WvT": np.asarray(L1_gnn_W_v).T,
    }
    arrays, args = {}, []
    for name, a in laid.items():
        a = np.ascontiguousarray(a)
        arrays[f"{name}_dram"] = a
        args.append(nc.dram_tensor(f"{name}_dram", a.shape, mb.dt.from_np(a.dtype), kind="ExternalInput").ap())
    args.append(nc.dram_tensor("out_dram", x.shape, mb.dt.float32, kind="ExternalOutput").ap())
    bass_gnn_pair(nc, *args)
    return run(nc, [arrays], core_ids=[0]).results[0]["out_dram"]
```

```python
from contextlib import ExitStack

import concourse.bass as bass
from concourse import mybir

P = 128
F32 = mybir.dt.float32
F32R = mybir.dt.float32r
ALU = mybir.AluOpType
ACT = mybir.ActivationFunctionType
AX_X = mybir.AxisListType.X

EPS = 1e-5
ROW_EPS = 1e-12
SLOPE = 0.2


def bass_gnn_pair(nc, xT, x, adjT, Wv, bv, aw, ab, Wk, bk, WqkT, WvT, out):
    B, N, D = x.shape
    NT = N // P
    DC = D // P
    HALF = N // 2
    NH = N // HALF
    TPH = NT // NH
    E = WqkT.shape[1] // 2
    SCALE = 1.0 / float(E) ** 0.5
    K = Wk.shape[0]
    UNITS = NH * NT
    GU = NH * NT
    XC = 4
    XCW = N // XC
    RING = 4
    QA = 2
    YL = D + 2
    assert K == 3 and D == 2 * P and HALF == 512 and 2 * E == P and XC == RING and UNITS == 16

    with ExitStack() as ctx:
        def sb(name, shape, dt=F32):
            return ctx.enter_context(nc.sbuf_tensor(name, shape, dt))

        def psum(name, shape):
            return ctx.enter_context(nc.psum_tensor(name, shape, F32))

        def sem(name):
            return ctx.enter_context(nc.semaphore(name))

        a_hi = sb("a_hi", [P, NT, N], F32R)
        a_lo = sb("a_lo", [P, NT, N], F32R)
        adj_a = sb("adj_a", [P, RING, HALF])
        stage = sb("stage", [P, RING, HALF])
        ag_hi = sb("ag_hi", [P, RING, HALF], F32R)
        ag_lo = sb("ag_lo", [P, RING, HALF], F32R)
        unit = sb("unit", [P, RING, HALF])
        xt_hi = sb("xt_hi", [P, DC, N], F32R)
        xt_lo = sb("xt_lo", [P, DC, N], F32R)
        y_cat = sb("y_cat", [P, NT, YL + D], F32R)
        z_cat = sb("z_cat", [P, NT, 2 * D], F32R)
        xw = sb("xw", [P, NT, 2 * D])
        xn = sb("xn", [P, NT, D])
        v_sb = sb("v_sb", [P, NT, D])
        k_cat = sb("k_cat", [P, NT, 2 * E], F32R)
        qT = sb("qT", [P, N])
        w2_hi, w2_lo = (sb(f"w2_{h}", [P, DC, D + 2], F32R) for h in ("hi", "lo"))
        w10_hi, w10_lo = (sb(f"w10_{h}", [P, DC, 2 * D], F32R) for h in ("hi", "lo"))
        wqq_hi, wqq_lo = (sb(f"wqq_{h}", [P, DC, 2 * E], F32R) for h in ("hi", "lo"))
        wkv_hi, wkv_lo = (sb(f"wkv_{h}", [P, DC, E + D], F32R) for h in ("hi", "lo"))
        ui_hi, ui_lo = (sb(f"ui_{h}", [P, DC, P], F32R) for h in ("hi", "lo"))
        bias_row = sb("bias_row", [P, D])
        ident = sb("ident", [P, P])
        ones = sb("ones", [P, P])
        neg_half = sb("neg_half", [P, TPH])
        u_cols = sb("u_cols", [P, 2, DC])
        u_pair = sb("u_pair", [P, 2])
        c_parts = sb("c_parts", [P, 3])
        c_col = sb("c_col", [P, 1])
        c_pair = sb("c_pair", [P, 2])
        ab_col = sb("ab_col", [P, 1])
        sj = sb("sj", [P, NT, 2])
        si_slope = sb("si_slope", [P, N])
        rsum = sb("rsum", [P, NT])
        rinv = sb("rinv", [P, NT])
        stats = sb("stats", [P, NT, 6])
        mv = sb("mv", [P, NT, 2])
        var_e = sb("var_e", [P, NT])
        n_mean = sb("n_mean", [P, NT])
        rstd = sb("rstd", [P, NT])
        shift = sb("shift", [P, NT])
        w_max = sb("w_max", [P, 1])
        g_max = sb("g_max", [1, 1])
        n_max = sb("n_max", [P, 1])
        e_col = sb("e_col", [P, NT])
        e_sum = sb("e_sum", [P, 1])
        t_inv = sb("t_inv", [P, 1])
        p_col = sb("p_col", [P, NT])

        x1t_hi = z_cat[:, 0:NT // 2, :].rearrange("p a b -> p (a b)").rearrange("p (c n) -> p c n", c=DC)
        x1t_lo = z_cat[:, NT // 2:NT, :].rearrange("p a b -> p (a b)").rearrange("p (c n) -> p c n", c=DC)

        hop = [psum(f"hop{i}", [P, 512]) for i in range(2)]
        si_b = [psum(f"si_b{i}", [P, HALF]) for i in range(NH)]
        gen = [psum(f"gen{i}", [P, 512]) for i in range(3)]
        misc = psum("misc", [P, 512])
        p_w = misc[:, 0:NT]
        p_maxT = misc[0:1, 64:64 + P]
        p_maxB = misc[:, 256:257]
        p_tot = misc[:, 320:321]

        U_XW2, U_XWA, U_X1T, U_QT, U_KV, U_XWB, USES = 0, 8, 10, 14, 16, 24, 30
        assert USES % 3 == 0

        def bank(idx):
            return gen[idx % 3]

        def xw_bank(nt):
            return bank(U_XWA + nt if nt < QA else U_XWB + nt - QA)

        s_par = sem("s_par")
        s_xt = [sem(f"s_xt{i}") for i in range(RING)]
        s_adja = [sem(f"s_adja{i}") for i in range(RING)]
        s_adjg = [sem(f"s_adjg{i}") for i in range(RING)]
        s_xn = [sem(f"s_xn{i}") for i in range(2)]
        s_out = [sem(f"s_out{i}") for i in range(2)]
        s_const = sem("s_const")
        s_id0 = sem("s_id0")
        s_setv = sem("s_setv")
        s_whi = sem("s_whi")
        s_wready = sem("s_wready")
        hop_done = sem("hop_done")
        si_done = sem("si_done")
        xw2_done = sem("xw2_done")
        xw10_done = sem("xw10_done")
        x1t_done = sem("x1t_done")
        qt_done = sem("qt_done")
        kv_done = sem("kv_done")
        g_done = sem("g_done")
        w_done = sem("w_done")
        maxT_done = sem("maxT_done")
        maxB_done = sem("maxB_done")
        tot_done = sem("tot_done")
        xt_hi_done = sem("xt_hi_done")
        z_hi_done = sem("z_hi_done")
        y_hi_done = sem("y_hi_done")
        si_slope_done = sem("si_slope_done")
        exp_done = sem("exp_done")
        x1_done = sem("x1_done")
        xw1_copied = sem("xw1_copied")
        x1t_hi_done = sem("x1t_hi_done")
        qt_copied = sem("qt_copied")
        ag_hi_done = sem("ag_hi_done")
        v_copied = sem("v_copied")
        p_exp_done = sem("p_exp_done")
        out_done = sem("out_done")
        rsum_done = sem("rsum_done")
        rinv_done = sem("rinv_done")
        z_done = sem("z_done")
        y_lo_done = sem("y_lo_done")
        h_done = sem("h_done")
        res_done = sem("res_done")
        stats_done = sem("stats_done")
        aggr_done = sem("aggr_done")
        var_done = sem("var_done")
        lrelu_done = sem("lrelu_done")
        alpha_done = sem("alpha_done")
        a_hi_done = sem("a_hi_done")
        xw0_copied = sem("xw0_copied")
        x1t_lo_done = sem("x1t_lo_done")
        k_lo_done = sem("k_lo_done")
        ag_lo_dve = sem("ag_lo_dve")
        qg_done = sem("qg_done")
        wmax_done = sem("wmax_done")
        gmax_done = sem("gmax_done")
        nmax_done = sem("nmax_done")
        tinv_done = sem("tinv_done")
        p_done = sem("p_done")
        y2_done = sem("y2_done")
        stats2_done = sem("stats2_done")
        aggr2_done = sem("aggr2_done")
        var2_done = sem("var2_done")
        xt_lo_done = sem("xt_lo_done")
        z_lo_done = sem("z_lo_done")
        a_lo_done = sem("a_lo_done")
        ag_lo_pool = sem("ag_lo_pool")
        rstd_done = sem("rstd_done")
        shift_done = sem("shift_done")
        rstd2_done = sem("rstd2_done")
        shift2_done = sem("shift2_done")

        def nth(batch, per_batch, c):
            return batch * per_batch + c

        def has_prior(batch):
            return not isinstance(batch, int) or batch > 0

        def run_slots(eng, slot):
            slot(0, True, False, False)
            slot(1, True, True, False)
            with eng.Fori(2, B) as s:
                slot(s, True, True, True)
            slot(B, False, True, True)
            slot(B + 1, False, False, True)

        flat_xw = xw[:, :, :].rearrange("p a b -> p (a b)")
        w2_raw = flat_xw[:, 0:512].rearrange("p (c n) -> p c n", c=DC)
        w10_raw = flat_xw[:, 512:1536].rearrange("p (c n) -> p c n", c=DC)
        wqk_raw = flat_xw[:, 1536:1792].rearrange("p (c n) -> p c n", c=DC)
        wvT_raw = flat_xw[:, 1792:2304].rearrange("p (c n) -> p c n", c=DC)
        flat_xn = xn[:, :, :].rearrange("p a b -> p (a b)")
        wv_nat = flat_xn[:, 0:DC * D].rearrange("p (c n) -> p c n", c=DC)
        aw_row = flat_xn[:, 512:1024]
        bv_row = flat_xn[:, 1024:1280]
        bk_rows = flat_xn[:, 1280:2048].rearrange("p (k n) -> p k n", k=K)
        N_PAR = 12

        block = ctx.enter_context(nc.Block())

        @block.sync
        def _(sp):
            def load_xt(f, c):
                if has_prior(f - 1):
                    sp.wait_ge(ag_lo_dve if c % 2 else ag_lo_pool, nth(f - 2, GU // 2, (GU - RING + c) // 2 + 1))
                elif not isinstance(f, int) or f == 1:
                    sp.wait_ge(xt_lo_done, nth(f - 1, XC, c + 1))
                sp.dma_start(stage[:, c, :].rearrange("p (c n) -> p c n", c=DC),
                             xT[f].rearrange("(c p) n -> p c n", p=P)[:, :, c * XCW:(c + 1) * XCW])\
                    .then_inc(s_xt[c], 16)

            def load_adj_a(f, u):
                if u >= RING:
                    sp.wait_ge(alpha_done, nth(f, UNITS, u - RING + 1))
                elif has_prior(f):
                    sp.wait_ge(alpha_done, nth(f - 1, UNITS, UNITS + u - RING + 1))
                h, jt = divmod(u, NT)
                sp.dma_start(adj_a[:, u % RING, :],
                             adjT[f].rearrange("(j p) i -> p j i", p=P)[:, jt, h * HALF:(h + 1) * HALF])\
                    .then_inc(s_adja[u % RING], 16)

            def load_adj_g(g, front, v):
                if v >= RING:
                    sp.wait_ge(ag_lo_dve if v % 2 else ag_lo_pool, nth(g, GU // 2, (v - RING) // 2 + 1))
                elif front:
                    sp.wait_ge(xt_lo_done, nth(g + 1, XC, v + 1))
                else:
                    sp.wait_ge(ag_lo_dve if v % 2 else ag_lo_pool, nth(g - 1, GU // 2, (GU - RING + v) // 2 + 1))
                mt, h = divmod(v, NH)
                sp.dma_start(stage[:, v % RING, :],
                             adjT[g].rearrange("(j p) i -> p j i", p=P)[:, mt, h * HALF:(h + 1) * HALF])\
                    .then_inc(s_adjg[v % RING], 16)

            for dst, src in ((w2_raw, Wk[2]), (w10_raw[:, :, 0:D], Wk[1]), (w10_raw[:, :, D:2 * D], Wk[0]),
                             (wqk_raw, WqkT), (wvT_raw, WvT), (wv_nat, Wv)):
                sp.dma_start(dst, src.rearrange("(c p) n -> p c n", p=P)).then_inc(s_par, 16)
            sp.dma_start(aw_row, aw.rearrange("a o -> o a").to_broadcast([P, 2 * D])).then_inc(s_par, 16)
            sp.dma_start(bv_row, bv.rearrange("(o a) -> o a", o=1).to_broadcast([P, D])).then_inc(s_par, 16)
            for k in range(K):
                sp.dma_start(bk_rows[:, k, :], bk[k:k + 1, :].to_broadcast([P, D])).then_inc(s_par, 16)
            sp.dma_start(ab_col[:, :], ab.rearrange("(o a) -> o a", o=1).to_broadcast([P, 1])).then_inc(s_par, 16)

            def slot(s, front, back, tail):
                f, g, t = s, s - 1, s - 2
                if front:
                    for c in range(XC):
                        load_xt(f, c)
                    for u in range(RING):
                        load_adj_a(f, u)
                if back:
                    for v in range(RING):
                        load_adj_g(g, front, v)
                if tail:
                    for h in range(2):
                        sp.wait_ge(out_done, nth(t, NT, (h + 1) * TPH))
                        sp.dma_start(out[t].rearrange("(n p) d -> p n d", p=P)[:, h * TPH:(h + 1) * TPH, :],
                                     xn[:, h * TPH:(h + 1) * TPH, :]).then_inc(s_out[h], 16)
                if back:
                    for h in range(2):
                        if tail:
                            sp.wait_ge(s_out[h], nth(t, 16, 16))
                        else:
                            sp.wait_ge(s_wready, 1)
                        sp.dma_start(xn[:, h * TPH:(h + 1) * TPH, :],
                                     x[g].rearrange("(n p) d -> p n d", p=P)[:, h * TPH:(h + 1) * TPH, :])\
                            .then_inc(s_xn[h], 16)
                if front:
                    for u in range(RING, 12):
                        load_adj_a(f, u)
                for j in range(4):
                    if back:
                        load_adj_g(g, front, 4 + 2 * j)
                        load_adj_g(g, front, 5 + 2 * j)
                    if front:
                        load_adj_a(f, 12 + j)
                if back:
                    for v in range(12, GU):
                        load_adj_g(g, front, v)

            run_slots(sp, slot)
            for h in range(2):
                sp.wait_ge(s_out[h], nth(B - 1, 16, 16))

        @block.gpsimd
        def _(pool):
            TT = nc.gpsimd.tensor_tensor
            nc.gpsimd.memset(ident[:, :], 0.0).then_inc(s_id0, 1)
            pool.wait_ge(s_id0, 1)
            nc.gpsimd.affine_select(out=ident[:, :], in_=ident[:, :], compare_op=ALU.not_equal, fill=1.0,
                                    base=0, pattern=[[-1, P]], channel_multiplier=1).then_inc(s_const, 1)
            nc.gpsimd.memset(neg_half[:, :], -0.5).then_inc(s_const, 1)

            def a_lo_unit(f, g, back, u):
                h, jt = divmod(u, NT)
                if back and jt == 0:
                    pool.wait_ge(hop_done, nth(g, 2 * NT, NT + TPH * (h + 1)))
                pool.wait_ge(a_hi_done, nth(f, UNITS, u + 1))
                cols = slice(h * HALF, (h + 1) * HALF)
                TT(a_lo[:, jt, cols], unit[:, u % RING, :], a_hi[:, jt, cols].bitcast(F32), ALU.subtract)\
                    .then_inc(a_lo_done, 1)

            def ag_lo_unit(g, v):
                pool.wait_ge(ag_hi_done, nth(g, GU, v + 1))
                TT(ag_lo[:, v % RING, :], stage[:, v % RING, :], ag_hi[:, v % RING, :].bitcast(F32), ALU.subtract)\
                    .then_inc(ag_lo_pool, 1)

            def norm_scale(b, h, var, rs, sh):
                half = slice(TPH * h, TPH * h + TPH)
                pool.wait_ge(var, nth(b, 2, h + 1))
                TT(rstd[:, half], var_e[:, half], neg_half[:, :], ALU.pow).then_inc(rs, 1)
                pool.wait_ge(rs, nth(b, 2, h + 1))
                TT(shift[:, half], n_mean[:, half], rstd[:, half], ALU.mult).then_inc(sh, 1)

            def slot(s, front, back, tail):
                f, g, t = s, s - 1, s - 2
                if front:
                    for c in range(XC):
                        pool.wait_ge(xt_hi_done, nth(f, XC, c + 1))
                        cols = slice(c * XCW, (c + 1) * XCW)
                        TT(xt_lo[:, :, cols], stage[:, c, :].rearrange("p (c n) -> p c n", c=DC),
                           xt_hi[:, :, cols].bitcast(F32), ALU.subtract).then_inc(xt_lo_done, 1)
                for it in range(NT):
                    if back:
                        pool.wait_ge(z_hi_done, nth(g, NT, it + 1))
                        TT(z_cat[:, it, D:2 * D], xw[:, it, 0:D], z_cat[:, it, 0:D].bitcast(F32), ALU.subtract)\
                            .then_inc(z_lo_done, 1)
                    if tail and it in (2, 4):
                        norm_scale(t, it // 2 - 1, var2_done, rstd2_done, shift2_done)
                if back:
                    if front:
                        a_lo_unit(f, g, back, 0)
                    norm_scale(g, 0, var_done, rstd_done, shift_done)
                    if front:
                        for u in range(1, 4):
                            a_lo_unit(f, g, back, u)
                    norm_scale(g, 1, var_done, rstd_done, shift_done)
                    if front:
                        a_lo_unit(f, g, back, 4)
                        a_lo_unit(f, g, back, 5)
                    ag_lo_unit(g, 0)
                    if front:
                        a_lo_unit(f, g, back, 6)
                        a_lo_unit(f, g, back, 7)
                elif front:
                    for u in range(8):
                        a_lo_unit(f, g, back, u)
                for j in range(8):
                    if back and j < 7:
                        ag_lo_unit(g, 2 * j + 2)
                    if front:
                        a_lo_unit(f, g, back, 8 + j)

            run_slots(pool, slot)

        @block.scalar
        def _(act):
            act.wait_ge(s_par, N_PAR * 16)
            nc.scalar.copy(w2_hi[:, :, 0:D], w2_raw)
            nc.scalar.copy(w10_hi[:, :, :], w10_raw)
            nc.scalar.copy(wqq_hi[:, :, 0:E], wqk_raw[:, :, 0:E])
            nc.scalar.copy(wqq_hi[:, :, E:2 * E], wqk_raw[:, :, 0:E])
            nc.scalar.copy(wkv_hi[:, :, 0:E], wqk_raw[:, :, E:2 * E])
            nc.scalar.copy(wkv_hi[:, :, E:E + D], wvT_raw).then_inc(s_whi, 1)

            def exp_unit(f, u):
                act.wait_ge(lrelu_done, nth(f, UNITS, u + 1))
                jt = u % NT
                nc.scalar.activation(unit[:, u % RING, :], unit[:, u % RING, :], ACT.Exp, bias=sj[:, jt, 1:2])\
                    .then_inc(exp_done, 1)

            def ag_hi_unit(g, v):
                if v >= RING:
                    act.wait_ge(g_done, nth(g, GU, v - RING + 1))
                elif has_prior(g):
                    act.wait_ge(g_done, nth(g - 1, GU, GU + v - RING + 1))
                act.wait_ge(s_adjg[v % RING], nth(g, 16 * (GU // RING), 16 * (v // RING + 1)))
                nc.scalar.copy(ag_hi[:, v % RING, :], stage[:, v % RING, :]).then_inc(ag_hi_done, 1)

            def normalise(b, h, sh, done):
                act.wait_ge(sh, nth(b, 2, h + 1))
                for n in range(TPH * h, TPH * h + TPH):
                    nc.scalar.activation(xn[:, n, :], xn[:, n, :], ACT.Identity, bias=shift[:, n:n + 1],
                                         scale=rstd[:, n:n + 1]).then_inc(done, 1)

            def xw1_copy(f, g, back, nt):
                act.wait_ge(xw10_done, nth(f, NT, nt + 1))
                nc.scalar.copy(xw[:, nt, 0:D], xw_bank(nt)[:, 0:D]).then_inc(xw1_copied, 1)

            def x1t_hi_copy(g, i):
                act.wait_ge(x1t_done, nth(g, 4, i + 1))
                if i == 0:
                    act.wait_ge(hop_done, nth(g, 2 * NT, 2 * NT))
                nc.scalar.copy(x1t_hi[:, :, 256 * i:256 * i + 256],
                               bank(U_X1T + i)[:, :].rearrange("p (c n) -> p c n", c=DC)).then_inc(x1t_hi_done, 1)

            def slot(s, front, back, tail):
                f, g, t = s, s - 1, s - 2
                if front:
                    if has_prior(f):
                        act.wait_ge(xw10_done, nth(f - 1, NT, NT))
                    for c in range(XC):
                        act.wait_ge(s_xt[c], nth(f, 16, 16))
                        nc.scalar.copy(xt_hi[:, :, c * XCW:(c + 1) * XCW],
                                       stage[:, c, :].rearrange("p (c n) -> p c n", c=DC)).then_inc(xt_hi_done, 1)
                for it in range(NT):
                    if back:
                        if it == 0 and has_prior(g):
                            act.wait_ge(kv_done, nth(g - 1, NT, NT))
                        act.wait_ge(z_done, nth(g, NT, it + 1))
                        nc.scalar.copy(z_cat[:, it, 0:D], xw[:, it, 0:D]).then_inc(z_hi_done, 1)
                    if tail and it in (3, 5):
                        normalise(t, (it - 3) // 2, shift2_done, out_done)
                if front:
                    for nt in range(NT):
                        act.wait_ge(xw2_done, nth(f, NT, nt + 1))
                        nc.scalar.copy(y_cat[:, nt, 0:D], bank(U_XW2 + nt)[:, 0:D]).then_inc(y_hi_done, 1)
                    if has_prior(f):
                        act.wait_ge(lrelu_done, nth(f - 1, UNITS, UNITS))
                    for h in range(NH):
                        act.wait_ge(si_done, nth(f, NH, h + 1))
                        nc.scalar.mul(si_slope[:, h * HALF:(h + 1) * HALF], si_b[h][:, :], SLOPE)\
                            .then_inc(si_slope_done, 1)
                    for u in range(3):
                        exp_unit(f, u)
                if back:
                    normalise(g, 0, shift_done, x1_done)
                if front:
                    exp_unit(f, 3)
                    for nt in range(QA):
                        xw1_copy(f, g, back, nt)
                if back:
                    normalise(g, 1, shift_done, x1_done)
                if front:
                    exp_unit(f, 4)
                if back:
                    ag_hi_unit(g, 0)
                    ag_hi_unit(g, 1)
                if front:
                    exp_unit(f, 5)
                for i in range(4):
                    if back:
                        x1t_hi_copy(g, i)
                    if front and i % 2 == 1:
                        exp_unit(f, 6 + i // 2)
                if back:
                    for h in range(NH):
                        act.wait_ge(qt_done, nth(g, NH, h + 1))
                        if h == 0 and has_prior(g):
                            act.wait_ge(w_done, nth(g - 1, 1, 1))
                        nc.scalar.copy(qT[:, h * HALF:(h + 1) * HALF], bank(U_QT + h)[:, :]).then_inc(qt_copied, 1)
                for j in range(8):
                    if back:
                        if j < 7:
                            ag_hi_unit(g, 2 * j + 2)
                            ag_hi_unit(g, 2 * j + 3)
                        act.wait_ge(kv_done, nth(g, NT, j + 1))
                        if j == 0 and has_prior(g):
                            act.wait_ge(g_done, nth(g - 1, GU, GU))
                            act.wait_ge(y2_done, nth(g - 1, NT, NT))
                        nc.scalar.copy(k_cat[:, j, 0:E], bank(U_KV + j)[:, 0:E])
                        nc.scalar.copy(v_sb[:, j, :], bank(U_KV + j)[:, E:E + D]).then_inc(v_copied, 1)
                    if front:
                        exp_unit(f, 8 + j)
                if front:
                    for nt in range(QA, NT - 1):
                        xw1_copy(f, g, back, nt)
                if back:
                    act.wait_ge(nmax_done, nth(g, 1, 1))
                    nc.scalar.activation(e_col[:, :], p_w, ACT.Exp, bias=n_max[:, :], scale=SCALE,
                                         accum_out=e_sum[:, :]).then_inc(p_exp_done, 1)
                if front:
                    xw1_copy(f, g, back, NT - 1)

            run_slots(act, slot)

        @block.vector
        def _(dve):
            V = nc.vector
            n_set = [0]

            def step(ins):
                n_set[0] += 1
                ins.then_inc(s_setv, 1)
                dve.wait_ge(s_setv, n_set[0])

            step(V.memset(ones[:, :], 1.0))
            for nt in range(NT):
                step(V.tensor_copy(y_cat[:, nt, D:YL], ones[:, 0:2]))
            dve.wait_ge(s_par, N_PAR * 16)
            prod = unit[:, 0, 0:D]
            for a in range(2):
                for c in range(DC):
                    step(V.tensor_tensor(prod, wv_nat[:, c, :], aw_row[:, a * D:(a + 1) * D], ALU.mult))
                    step(V.tensor_reduce(u_cols[:, a, c:c + 1], prod, AX_X, ALU.add))
                step(V.tensor_tensor(prod, bv_row, aw_row[:, a * D:(a + 1) * D], ALU.mult))
                step(V.tensor_reduce(c_parts[:, a:a + 1], prod, AX_X, ALU.add))
            step(V.tensor_copy(c_parts[:, 2:3], ab_col[:, :]))
            step(V.tensor_reduce(c_col[:, :], c_parts[:, :], AX_X, ALU.add))
            step(V.tensor_scalar(c_pair[:, 0:1], c_col[:, :], 1.0 - SLOPE, None, ALU.mult))
            step(V.tensor_scalar(c_pair[:, 1:2], c_col[:, :], SLOPE, None, ALU.mult))
            step(V.tensor_tensor(prod, bk_rows[:, 0, :], bk_rows[:, 1, :], ALU.add))
            step(V.tensor_tensor(bias_row[:, :], prod, bk_rows[:, 2, :], ALU.add))
            for c in range(DC):
                step(V.tensor_scalar(u_pair[:, 0:1], u_cols[:, 0, c:c + 1], 1.0 - SLOPE, None, ALU.mult))
                step(V.tensor_scalar(u_pair[:, 1:2], u_cols[:, 0, c:c + 1], SLOPE, None, ALU.mult))
                step(V.tensor_copy(w2_hi[:, c, D:D + 2], u_pair[:, :]))
                step(V.tensor_tensor(w2_lo[:, c, D:D + 2], u_pair[:, :], w2_hi[:, c, D:D + 2].bitcast(F32),
                                     ALU.subtract))
                ub = prod[:, 0:P]
                step(V.tensor_scalar(ub, ones[:, :], u_cols[:, 1, c:c + 1], None, ALU.mult))
                step(V.tensor_copy(ui_hi[:, c, :], ub))
                step(V.tensor_tensor(ui_lo[:, c, :], ub, ui_hi[:, c, :].bitcast(F32), ALU.subtract))
            dve.wait_ge(s_whi, 1)
            for raw, hi, lo in ((w2_raw, w2_hi[:, :, 0:D], w2_lo[:, :, 0:D]),
                                (w10_raw, w10_hi[:, :, :], w10_lo[:, :, :]),
                                (wqk_raw[:, :, 0:E], wqq_hi[:, :, 0:E], wqq_lo[:, :, 0:E]),
                                (wqk_raw[:, :, 0:E], wqq_hi[:, :, E:2 * E], wqq_lo[:, :, E:2 * E]),
                                (wqk_raw[:, :, E:2 * E], wkv_hi[:, :, 0:E], wkv_lo[:, :, 0:E]),
                                (wvT_raw, wkv_hi[:, :, E:E + D], wkv_lo[:, :, E:E + D])):
                last = V.tensor_tensor(lo, raw, hi.bitcast(F32), ALU.subtract)
            last.then_inc(s_wready, 1)
            dve.wait_ge(s_wready, 1)

            def lrelu_unit(f, u):
                h, jt = divmod(u, NT)
                if u >= RING:
                    dve.wait_ge(a_lo_done, nth(f, UNITS, u - RING + 1))
                elif has_prior(f):
                    dve.wait_ge(a_lo_done, nth(f - 1, UNITS, UNITS + u - RING + 1))
                if u == 0:
                    dve.wait_ge(y_lo_done, nth(f, NT, NT))
                if jt == 0:
                    dve.wait_ge(si_slope_done, nth(f, NH, h + 1))
                V.scalar_tensor_tensor(unit[:, u % RING, :], si_b[h][:, :], sj[:, jt, 0:1],
                                       si_slope[:, h * HALF:(h + 1) * HALF], ALU.add, ALU.max)\
                    .then_inc(lrelu_done, 1)

            def alpha_unit(f, g, back, u):
                h, jt = divmod(u, NT)
                if u == 0:
                    lrelu_unit(f, 0)
                    lrelu_unit(f, 1)
                dve.wait_ge(exp_done, nth(f, UNITS, u + 1))
                dve.wait_ge(s_adja[u % RING], nth(f, 16 * (UNITS // RING), 16 * (u // RING + 1)))
                V.tensor_tensor(unit[:, u % RING, :], unit[:, u % RING, :], adj_a[:, u % RING, :], ALU.mult)\
                    .then_inc(alpha_done, 1)
                if u + 2 < UNITS:
                    lrelu_unit(f, u + 2)
                dve.wait_ge(alpha_done, nth(f, UNITS, u + 1))
                if back and jt == 0:
                    dve.wait_ge(hop_done, nth(g, 2 * NT, NT + TPH * (h + 1)))
                V.tensor_copy(a_hi[:, jt, h * HALF:(h + 1) * HALF], unit[:, u % RING, :]).then_inc(a_hi_done, 1)

            def xw0_copy(f, nt):
                dve.wait_ge(xw1_copied, nth(f, NT, nt + 1))
                V.tensor_tensor(xw[:, nt, D:2 * D], xw_bank(nt)[:, D:2 * D], bias_row[:, :], ALU.add)\
                    .then_inc(xw0_copied, 1)

            def moments(b, h, aggr, var):
                half = slice(TPH * h, TPH * h + TPH)
                V.memset(var_e[:, half], EPS)
                for n in range(TPH * h, TPH * h + TPH):
                    V.bn_aggr(mv[:, n, :], stats[:, n, :]).then_inc(aggr, 1)
                dve.wait_ge(aggr, nth(b, NT, TPH * h + TPH))
                V.tensor_scalar(n_mean[:, half], mv[:, half, 0], -1.0, None, ALU.mult)
                V.tensor_tensor(var_e[:, half], mv[:, half, 1], var_e[:, half], ALU.add).then_inc(var, 1)

            def y2_tile(t, n):
                V.scalar_tensor_tensor(xn[:, n, :], v_sb[:, n, :], p_col[:, n:n + 1], xn[:, n, :],
                                       ALU.mult, ALU.add).then_inc(y2_done, 1)
                dve.wait_ge(y2_done, nth(t, NT, n + 1))
                V.bn_stats(stats[:, n, :], xn[:, n, :]).then_inc(stats2_done, 1)

            def ag_lo_unit(g, v):
                dve.wait_ge(ag_hi_done, nth(g, GU, v + 1))
                V.tensor_tensor(ag_lo[:, v % RING, :], stage[:, v % RING, :], ag_hi[:, v % RING, :].bitcast(F32),
                                ALU.subtract).then_inc(ag_lo_dve, 1)

            def slot(s, front, back, tail):
                f, g, t = s, s - 1, s - 2
                for it in range(NT):
                    if back:
                        col = slice(it, it + 1)
                        dve.wait_ge(hop_done, nth(g, 2 * NT, it + 1))
                        V.tensor_scalar(rsum[:, col], hop[it % 2][:, D:D + 1], ROW_EPS, None, ALU.add)\
                            .then_inc(rsum_done, 1)
                        dve.wait_ge(rsum_done, nth(g, NT, it + 1))
                        V.reciprocal(rinv[:, col], rsum[:, col]).then_inc(rinv_done, 1)
                        dve.wait_ge(rinv_done, nth(g, NT, it + 1))
                        V.scalar_tensor_tensor(xw[:, it, 0:D], hop[it % 2][:, 0:D], rinv[:, col],
                                               xw[:, it, 0:D], ALU.mult, ALU.add).then_inc(z_done, 1)
                    if tail and it == 0:
                        dve.wait_ge(p_done, nth(t, 1, 1))
                    if tail and it < 4:
                        y2_tile(t, 2 * it)
                        y2_tile(t, 2 * it + 1)
                        if it % 2:
                            dve.wait_ge(stats2_done, nth(t, NT, 2 * it + 2))
                            moments(t, it // 2, aggr2_done, var2_done)
                if front:
                    for nt in range(NT):
                        b = bank(U_XW2 + nt)
                        dve.wait_ge(y_hi_done, nth(f, NT, nt + 1))
                        V.tensor_tensor(sj[:, nt, :], b[:, D:D + 2], c_pair[:, :], ALU.add)
                        V.tensor_tensor(y_cat[:, nt, YL:YL + D], b[:, 0:D], y_cat[:, nt, 0:D].bitcast(F32),
                                        ALU.subtract).then_inc(y_lo_done, 1)
                if back:
                    for it in range(NT):
                        dve.wait_ge(hop_done, nth(g, 2 * NT, NT + it + 1))
                        V.scalar_tensor_tensor(xw[:, it, D:2 * D], hop[it % 2][:, 0:D], rinv[:, it:it + 1],
                                               xw[:, it, D:2 * D], ALU.mult, ALU.add).then_inc(h_done, 1)
                        if it % TPH == 0:
                            dve.wait_ge(s_xn[it // TPH], nth(g, 16, 16))
                        dve.wait_ge(h_done, nth(g, NT, it + 1))
                        V.scalar_tensor_tensor(xn[:, it, :], xw[:, it, D:2 * D], 0.0, xn[:, it, :],
                                               ALU.max, ALU.add).then_inc(res_done, 1)
                        dve.wait_ge(res_done, nth(g, NT, it + 1))
                        V.bn_stats(stats[:, it, :], xn[:, it, :]).then_inc(stats_done, 1)
                        if front and it >= 4:
                            alpha_unit(f, g, back, it - 4)
                        if it == 4:
                            dve.wait_ge(stats_done, nth(g, NT, TPH))
                            moments(g, 0, aggr_done, var_done)
                        if it == 7:
                            dve.wait_ge(stats_done, nth(g, NT, NT))
                            moments(g, 1, aggr_done, var_done)
                elif front:
                    for u in range(4):
                        alpha_unit(f, g, back, u)
                if front:
                    for nt in range(QA):
                        xw0_copy(f, nt)
                    alpha_unit(f, g, back, 4)
                    alpha_unit(f, g, back, 5)
                if back:
                    ag_lo_unit(g, 1)
                for i in range(4):
                    if back:
                        cols = slice(256 * i, 256 * i + 256)
                        dve.wait_ge(x1t_hi_done, nth(g, 4, i + 1))
                        V.tensor_tensor(x1t_lo[:, :, cols], bank(U_X1T + i)[:, :].rearrange("p (c n) -> p c n", c=DC),
                                        x1t_hi[:, :, cols].bitcast(F32), ALU.subtract).then_inc(x1t_lo_done, 1)
                    if front and i % 2 == 1:
                        alpha_unit(f, g, back, 6 + i // 2)
                for j in range(8):
                    if back:
                        if j < 7:
                            ag_lo_unit(g, 2 * j + 3)
                        dve.wait_ge(v_copied, nth(g, NT, j + 1))
                        V.tensor_tensor(k_cat[:, j, E:2 * E], bank(U_KV + j)[:, 0:E], k_cat[:, j, 0:E].bitcast(F32),
                                        ALU.subtract).then_inc(k_lo_done, 1)
                    if front:
                        alpha_unit(f, g, back, 8 + j)
                if back:
                    for h in range(NH):
                        cols = slice(h * HALF, (h + 1) * HALF)
                        dve.wait_ge(g_done, nth(g, GU, GU - 1 + h))
                        if h == 0:
                            dve.wait_ge(qt_copied, nth(g, NH, NH))
                        V.tensor_tensor(qT[:, cols], hop[h][:, :], qT[:, cols], ALU.mult).then_inc(qg_done, 1)
                if front:
                    xw0_copy(f, 2)
                    xw0_copy(f, 3)
                if back:
                    dve.wait_ge(w_done, nth(g, 1, 1))
                    V.tensor_reduce(w_max[:, :], p_w, AX_X, ALU.max).then_inc(wmax_done, 1)
                if front:
                    xw0_copy(f, 4)
                if back:
                    dve.wait_ge(maxT_done, nth(g, 1, 1))
                    V.tensor_reduce(g_max[:, :], p_maxT, AX_X, ALU.max).then_inc(gmax_done, 1)
                if front:
                    xw0_copy(f, 5)
                if back:
                    dve.wait_ge(maxB_done, nth(g, 1, 1))
                    V.tensor_scalar(n_max[:, :], p_maxB, -SCALE, None, ALU.mult).then_inc(nmax_done, 1)
                if front:
                    xw0_copy(f, 6)
                    xw0_copy(f, 7)
                if back:
                    dve.wait_ge(tot_done, nth(g, 1, 1))
                    V.reciprocal(t_inv[:, :], p_tot).then_inc(tinv_done, 1)
                    dve.wait_ge(tinv_done, nth(g, 1, 1))
                    V.tensor_scalar(p_col[:, :], e_col[:, :], t_inv[:, :], None, ALU.mult).then_inc(p_done, 1)

            run_slots(dve, slot)

        @block.tensor
        def _(pe):
            mm = nc.tensor.matmul

            def mm3(o, l_hi, l_lo, r_hi, r_lo, first, last):
                mm(o, l_hi, r_hi, start=first, stop=False)
                mm(o, l_hi, r_lo, start=False, stop=False)
                return mm(o, l_lo, r_hi, start=False, stop=last)

            pe.wait_ge(s_const, 1)
            pe.wait_ge(s_wready, 1)

            def hop1_tile(g, it):
                if it >= 2:
                    pe.wait_ge(z_done, nth(g, NT, it - 1))
                elif has_prior(g):
                    pe.wait_ge(qg_done, nth(g - 1, NH, it + 1))
                o, rows = hop[it % 2], slice(it * P, (it + 1) * P)
                for jt in range(NT):
                    mm(o[:, 0:YL], a_hi[:, jt, rows], y_cat[:, jt, 0:YL], start=(jt == 0), stop=False)
                    mm(o[:, 0:D], a_hi[:, jt, rows], y_cat[:, jt, YL:YL + D], start=False, stop=False)
                    last = mm(o[:, 0:YL], a_lo[:, jt, rows], y_cat[:, jt, 0:YL], start=False, stop=(jt == NT - 1))
                last.then_inc(hop_done, 1)

            def hop2_tile(g, it):
                if it >= 2:
                    pe.wait_ge(h_done, nth(g, NT, it - 1))
                else:
                    pe.wait_ge(z_done, nth(g, NT, NT + it - 1))
                o, rows = hop[it % 2], slice(it * P, (it + 1) * P)
                for jt in range(NT):
                    last = mm3(o[:, 0:D], a_hi[:, jt, rows], a_lo[:, jt, rows], z_cat[:, jt, 0:D],
                               z_cat[:, jt, D:2 * D], jt == 0, jt == NT - 1)
                last.then_inc(hop_done, 1)

            def xw10(f, back, nt):
                if nt < QA:
                    pe.wait_ge(y_lo_done, nth(f, NT, NT - 2 + nt))
                elif nt >= QA + 3:
                    pe.wait_ge(xw0_copied, nth(f, NT, nt - 2))
                elif back:
                    pe.wait_ge(k_lo_done, nth(f - 1, NT, NT - 2 + nt - QA))
                elif nt == QA:
                    pe.wait_ge(xw0_copied, nth(f, NT, QA))
                    pe.wait_ge(y_lo_done, nth(f, NT, NT))
                rows = slice(nt * P, (nt + 1) * P)
                for c in range(DC):
                    last = mm3(xw_bank(nt)[:, :], xt_hi[:, c, rows], xt_lo[:, c, rows],
                               w10_hi[:, c, :], w10_lo[:, c, :], c == 0, c == DC - 1)
                last.then_inc(xw10_done, 1)

            def kv_tile(g, j):
                if j >= 3:
                    pe.wait_ge(k_lo_done, nth(g, NT, j - 2))
                elif j:
                    pe.wait_ge(qt_copied, nth(g, NH, j))
                rows = slice(j * P, (j + 1) * P)
                for c in range(DC):
                    last = mm3(bank(U_KV + j)[:, 0:E + D], x1t_hi[:, c, rows], x1t_lo[:, c, rows],
                               wkv_hi[:, c, :], wkv_lo[:, c, :], c == 0, c == DC - 1)
                last.then_inc(kv_done, 1)

            def g_tile(g, mt):
                pe.wait_ge(k_lo_done, nth(g, NT, mt + 1))
                for h in range(NH):
                    v = NH * mt + h
                    if mt == 0:
                        pe.wait_ge(h_done, nth(g, NT, NT - 1 + h))
                    if v % 2:
                        pe.wait_ge(ag_lo_dve, nth(g, GU // 2, v // 2 + 1))
                    else:
                        pe.wait_ge(ag_lo_pool, nth(g, GU // 2, v // 2 + 1))
                    o, hi, lo = hop[h], ag_hi[:, v % RING, :], ag_lo[:, v % RING, :]
                    if mt < NT - 1:
                        mm(o[:, :], k_cat[:, mt, :], hi, start=(mt == 0), stop=False)
                        mm(o[0:E, :], k_cat[:, mt, 0:E], lo, start=False, stop=False).then_inc(g_done, 1)
                    else:
                        mm(o[0:E, :], k_cat[:, mt, 0:E], lo, start=False, stop=False)
                        mm(o[:, :], k_cat[:, mt, :], hi, start=False, stop=True).then_inc(g_done, 1)

            def slot(s, front, back, tail):
                f, g = s, s - 1
                if back:
                    pe.wait_ge(y_lo_done, nth(g, NT, NT))
                    for it in range(NT):
                        if it % TPH == 0:
                            pe.wait_ge(a_lo_done, nth(g, UNITS, NT * (it // TPH + 1)))
                        hop1_tile(g, it)
                if front:
                    for h in range(NH):
                        pe.wait_ge(xt_lo_done, nth(f, XC, (h + 1) * XC // NH))
                        if h == 0 and has_prior(f):
                            pe.wait_ge(lrelu_done, nth(f - 1, UNITS, UNITS))
                        for c in range(DC):
                            cols = slice(h * HALF, (h + 1) * HALF)
                            last = mm3(si_b[h][:, :], ui_hi[:, c, :], ui_lo[:, c, :], xt_hi[:, c, cols],
                                       xt_lo[:, c, cols], c == 0, c == DC - 1)
                        last.then_inc(si_done, 1)
                    for nt in range(NT):
                        if nt >= 3:
                            pe.wait_ge(y_lo_done, nth(f, NT, nt - 2))
                        elif has_prior(f):
                            pe.wait_ge(xw0_copied, nth(f - 1, NT, NT - 2 + nt))
                        rows = slice(nt * P, (nt + 1) * P)
                        for c in range(DC):
                            last = mm3(bank(U_XW2 + nt)[:, 0:D + 2], xt_hi[:, c, rows], xt_lo[:, c, rows],
                                       w2_hi[:, c, :], w2_lo[:, c, :], c == 0, c == DC - 1)
                        last.then_inc(xw2_done, 1)
                if back:
                    for it in range(NT):
                        if it == 0:
                            pe.wait_ge(z_lo_done, nth(g, NT, NT))
                        hop2_tile(g, it)
                if front:
                    for nt in range(QA):
                        xw10(f, back, nt)
                if back:
                    for i in range(4):
                        if i == 3:
                            pe.wait_ge(x1t_lo_done, nth(g, 4, 1))
                        elif not front:
                            pe.wait_ge(xw0_copied, nth(f - 1, NT, NT))
                        elif i == 0:
                            pe.wait_ge(y_lo_done, nth(f, NT, NT))
                        else:
                            pe.wait_ge(xw0_copied, nth(f, NT, i))
                        pe.wait_ge(x1_done, nth(g, NT, 2 * i + 2))
                        b = bank(U_X1T + i)
                        for c in range(DC):
                            for j in range(2):
                                last = nc.tensor.transpose(b[:, c * 256 + j * P:c * 256 + (j + 1) * P],
                                                           xn[:, 2 * i + j, c * P:(c + 1) * P], ident[:, :])
                        last.then_inc(x1t_done, 1)
                    for h in range(NH):
                        pe.wait_ge(x1t_lo_done, nth(g, 4, 2 * h + 2))
                        cols = slice(h * HALF, (h + 1) * HALF)
                        for c in range(DC):
                            last = mm3(bank(U_QT + h)[:, :], wqq_hi[:, c, :], wqq_lo[:, c, :], x1t_hi[:, c, cols],
                                       x1t_lo[:, c, cols], c == 0, c == DC - 1)
                        last.then_inc(qt_done, 1)
                    kv_tile(g, 0)
                    kv_tile(g, 1)
                    for mt in range(NT):
                        if mt + 2 < NT:
                            kv_tile(g, mt + 2)
                        g_tile(g, mt)
                if front:
                    for nt in range(QA, QA + 2):
                        xw10(f, back, nt)
                if back:
                    pe.wait_ge(qg_done, nth(g, NH, NH))
                    if has_prior(g):
                        pe.wait_ge(tinv_done, nth(g - 1, 1, 1))
                    for it in range(NT):
                        last = mm(misc[:, it:it + 1], qT[:, it * P:(it + 1) * P], ones[:, 0:1], start=True, stop=True)
                    last.then_inc(w_done, 1)
                if front:
                    xw10(f, back, QA + 2)
                if back:
                    pe.wait_ge(wmax_done, nth(g, 1, 1))
                    nc.tensor.transpose(p_maxT, w_max[:, :], ident[:, :]).then_inc(maxT_done, 1)
                if front:
                    xw10(f, back, QA + 3)
                if back:
                    pe.wait_ge(gmax_done, nth(g, 1, 1))
                    mm(p_maxB, ones[0:1, :], g_max[:, :], start=True, stop=True).then_inc(maxB_done, 1)
                if front:
                    xw10(f, back, QA + 4)
                    xw10(f, back, QA + 5)
                if back:
                    pe.wait_ge(p_exp_done, nth(g, 1, 1))
                    mm(p_tot, ones[:, :], e_sum[:, :], start=True, stop=True).then_inc(tot_done, 1)

            run_slots(pe, slot)


def kernel(x, adj, L0_gnn_Wv, L0_gnn_bv, L0_gnn_aw, L0_gnn_ab, L0_gnn_Wk, L0_gnn_bk, L1_gnn_W_qk, L1_gnn_W_v):
    import numpy as np
    import concourse.bacc as bacc
    from concourse import mybir as mb
    from concourse.bass_utils import run_bass_kernel_spmd as run

    nc = bacc.Bacc("TRN2", target_bir_lowering=False, num_devices=1, dynamic_dma_scratch_size=1024)
    laid = {
        "xT": np.asarray(x).transpose(0, 2, 1), "x": x, "adjT": np.asarray(adj).transpose(0, 2, 1),
        "Wv": L0_gnn_Wv, "bv": L0_gnn_bv, "aw": L0_gnn_aw, "ab": L0_gnn_ab, "Wk": L0_gnn_Wk, "bk": L0_gnn_bk,
        "WqkT": np.asarray(L1_gnn_W_qk).T, "WvT": np.asarray(L1_gnn_W_v).T,
    }
    arrays, args = {}, []
    for name, a in laid.items():
        a = np.ascontiguousarray(a)
        arrays[f"{name}_dram"] = a
        args.append(nc.dram_tensor(f"{name}_dram", a.shape, mb.dt.from_np(a.dtype), kind="ExternalInput").ap())
    args.append(nc.dram_tensor("out_dram", x.shape, mb.dt.float32, kind="ExternalOutput").ap())
    bass_gnn_pair(nc, *args)
    return run(nc, [arrays], core_ids=[0]).results[0]["out_dram"]
```

```python
from contextlib import ExitStack

import concourse.bass as bass
from concourse import mybir

P = 128
F32 = mybir.dt.float32
F32R = mybir.dt.float32r
ALU = mybir.AluOpType
ACT = mybir.ActivationFunctionType
AX_X = mybir.AxisListType.X

EPS = 1e-5
ROW_EPS = 1e-12
SLOPE = 0.2


def bass_gnn_pair(nc, xT, x, adj, adjT, Wv, bv, aw, ab, Wk, bk, WqkT, WvT, out):
    B, N, D = x.shape
    NT = N // P
    DC = D // P
    HALF = N // 2
    NH = N // HALF
    TPH = NT // NH
    E = WqkT.shape[1] // 2
    SCALE = 1.0 / float(E) ** 0.5
    K = Wk.shape[0]
    UNITS = NH * NT
    SU = NH * NT
    XC = 4
    XCW = N // XC
    RING = 4
    UR = 10
    YL = D + 2
    LC = 4
    assert K == 3 and D == 2 * P and HALF == 512 and 2 * E == P and XC == RING and UNITS == 16

    with ExitStack() as ctx:
        def sb(name, shape, dt=F32):
            return ctx.enter_context(nc.sbuf_tensor(name, shape, dt))

        def psum(name, shape):
            return ctx.enter_context(nc.psum_tensor(name, shape, F32))

        def sem(name):
            return ctx.enter_context(nc.semaphore(name))

        a_hi = sb("a_hi", [P, NT, N], F32R)
        a_lo = sb("a_lo", [P, NT, N], F32R)
        adj_a = sb("adj_a", [P, RING, HALF])
        stage = sb("stage", [P, RING, HALF])
        unit = sb("unit", [P, UR, HALF])
        xt_hi = sb("xt_hi", [P, DC, N], F32R)
        xt_lo = sb("xt_lo", [P, DC, N], F32R)
        y_cat = sb("y_cat", [P, NT, YL + D], F32R)
        z_cat = sb("z_cat", [P, NT, 2 * D], F32R)
        xw = sb("xw", [P, NT, 2 * D])
        xn = sb("xn", [P, NT, D])
        v_sb = sb("v_sb", [P, NT, D])
        q_hi = sb("q_hi", [P, N], F32R)
        q_lo = sb("q_lo", [E, N], F32R)
        k_cat = sb("k_cat", [P, N], F32R)
        w2_hi, w2_lo = (sb(f"w2_{h}", [P, DC, D + LC], F32R) for h in ("hi", "lo"))
        w10_hi, w10_lo = (sb(f"w10_{h}", [P, DC, 2 * D], F32R) for h in ("hi", "lo"))
        wqq_hi, wqq_lo = (sb(f"wqq_{h}", [P, DC, 2 * E], F32R) for h in ("hi", "lo"))
        wkk_hi, wkk_lo = (sb(f"wkk_{h}", [P, DC, 2 * E], F32R) for h in ("hi", "lo"))
        wv_hi, wv_lo = (sb(f"wv_{h}", [P, DC, D], F32R) for h in ("hi", "lo"))
        bias_row = sb("bias_row", [P, D])
        ident = sb("ident", [P, P])
        ones = sb("ones", [P, P])
        neg_half = sb("neg_half", [P, TPH])
        u_cols = sb("u_cols", [P, 2, DC])
        u_log = sb("u_log", [P, DC, LC])
        c_parts = sb("c_parts", [P, 3])
        c_col = sb("c_col", [P, 1])
        c_add = sb("c_add", [P, LC])
        ab_col = sb("ab_col", [P, 1])
        logit = sb("logit", [P, NT, LC])
        si_slope = sb("si_slope", [P, N])
        rsum = sb("rsum", [P, NT])
        rinv = sb("rinv", [P, NT])
        stats = sb("stats", [P, NT, 6])
        mv = sb("mv", [P, NT, 2])
        var_e = sb("var_e", [P, NT])
        n_mean = sb("n_mean", [P, NT])
        rstd = sb("rstd", [P, NT])
        shift = sb("shift", [P, NT])
        w_part = sb("w_part", [P, NT, NH])
        w_col = sb("w_col", [P, NT])
        w_max = sb("w_max", [P, 1])
        g_max = sb("g_max", [1, 1])
        n_max = sb("n_max", [P, 1])
        e_col = sb("e_col", [P, NT])
        e_sum = sb("e_sum", [P, 1])
        t_inv = sb("t_inv", [P, 1])
        p_col = sb("p_col", [P, NT])

        x1t_hi = z_cat[:, 0:NT // 2, :].rearrange("p a b -> p (a b)").rearrange("p (c n) -> p c n", c=DC)
        x1t_lo = z_cat[:, NT // 2:NT, :].rearrange("p a b -> p (a b)").rearrange("p (c n) -> p c n", c=DC)

        hop = [psum(f"hop{i}", [P, 512]) for i in range(2)]
        si_b = [psum(f"si_b{i}", [P, HALF]) for i in range(NH)]
        gen = [psum(f"gen{i}", [P, 512]) for i in range(3)]
        score = [*hop, *si_b]
        misc = psum("misc", [P, 512])
        p_maxT = misc[0:1, 64:64 + P]
        p_maxB = misc[:, 256:257]
        p_tot = misc[:, 320:321]

        U_XW2, U_XW10, U_QK, U_V = 0, 8, 16, 20

        def bank(idx):
            return gen[idx % 3]

        UNITS_AT_HOP2 = ((0,), (1,), (2, 3), (4,), (5,), (6, 7), (8,), (9,))
        LO_AT_HOP2 = ((), (), (), (), (0, 1), (2,), (3,), (4,))
        HI_ON_DVE = range(8, 14)
        XW_AT_FIRST = (0, 1, 2, 4, 6, 8, 9, 10)
        N_DVE = len(HI_ON_DVE)
        LO_LEFT = sum(len(us) for us in LO_AT_HOP2)

        s_par_logit = sem("s_par_logit")
        s_par_rest = sem("s_par_rest")
        s_xt = [sem(f"s_xt{i}") for i in range(RING)]
        s_adja = [sem(f"s_adja{i}") for i in range(RING)]
        s_adjs = [sem(f"s_adjs{i}") for i in range(RING)]
        s_xn = [sem(f"s_xn{i}") for i in range(NH)]
        s_out = [sem(f"s_out{i}") for i in range(NH)]
        s_const = sem("s_const")
        s_id0 = sem("s_id0")
        s_setv = sem("s_setv")
        s_bias = sem("s_bias")
        s_w2_hi = sem("s_w2_hi")
        s_w2_ready = sem("s_w2_ready")
        s_w10_hi = sem("s_w10_hi")
        s_wqkv_hi = sem("s_wqkv_hi")
        s_w10_ready = sem("s_w10_ready")
        s_wqkv_ready = sem("s_wqkv_ready")
        hop_done = sem("hop_done")
        si_done = sem("si_done")
        xw2_done = sem("xw2_done")
        xw10_done = sem("xw10_done")
        x1t_done = sem("x1t_done")
        qk_done = sem("qk_done")
        v_done = sem("v_done")
        s_done = sem("s_done")
        maxT_done = sem("maxT_done")
        maxB_done = sem("maxB_done")
        tot_done = sem("tot_done")
        xt_hi_done = sem("xt_hi_done")
        z_hi_done = sem("z_hi_done")
        y_hi_done = sem("y_hi_done")
        si_slope_done = sem("si_slope_done")
        exp_done = sem("exp_done")
        relu_done = sem("relu_done")
        xw_copied = sem("xw_copied")
        x1t_hi_done = sem("x1t_hi_done")
        qk_hi_done = sem("qk_hi_done")
        a_hi_act = sem("a_hi_act")
        v_copied = sem("v_copied")
        p_exp_done = sem("p_exp_done")
        out_done = sem("out_done")
        rsum_done = sem("rsum_done")
        rinv_done = sem("rinv_done")
        z_done = sem("z_done")
        y_lo_done = sem("y_lo_done")
        h_done = sem("h_done")
        stats_done = sem("stats_done")
        aggr_done = sem("aggr_done")
        var_done = sem("var_done")
        x1_done = sem("x1_done")
        lrelu_done = sem("lrelu_done")
        a_hi_dve = sem("a_hi_dve")
        alpha_done = sem("alpha_done")
        x1t_lo_done = sem("x1t_lo_done")
        qk_lo_done = sem("qk_lo_done")
        w_part_done = sem("w_part_done")
        w_col_done = sem("w_col_done")
        wmax_done = sem("wmax_done")
        gmax_done = sem("gmax_done")
        nmax_done = sem("nmax_done")
        tinv_done = sem("tinv_done")
        p_done = sem("p_done")
        y2_done = sem("y2_done")
        stats2_done = sem("stats2_done")
        aggr2_done = sem("aggr2_done")
        var2_done = sem("var2_done")
        xt_lo_done = sem("xt_lo_done")
        z_lo_done = sem("z_lo_done")
        a_lo_done = sem("a_lo_done")
        res_done = sem("res_done")
        bias_done = sem("bias_done")
        rstd_done = sem("rstd_done")
        shift_done = sem("shift_done")
        rstd2_done = sem("rstd2_done")
        shift2_done = sem("shift2_done")

        def nth(batch, per_batch, c):
            return batch * per_batch + c

        def has_prior(batch):
            return not isinstance(batch, int) or batch > 0

        def run_slots(eng, slot):
            slot(0, True, False, False)
            slot(1, True, True, False)
            with eng.Fori(2, B) as s:
                slot(s, True, True, True)
            slot(B, False, True, True)
            slot(B + 1, False, False, True)

        flat_xw = xw[:, :, :].rearrange("p a b -> p (a b)")
        w2_raw = flat_xw[:, 0:512].rearrange("p (c n) -> p c n", c=DC)
        w10_raw = flat_xw[:, 512:1536].rearrange("p (c n) -> p c n", c=DC)
        flat_v = v_sb[:, :, :].rearrange("p a b -> p (a b)")
        wqk_raw = flat_v[:, 0:256].rearrange("p (c n) -> p c n", c=DC)
        wvT_raw = flat_v[:, 256:768].rearrange("p (c n) -> p c n", c=DC)
        flat_xn = xn[:, :, :].rearrange("p a b -> p (a b)")
        wv_nat = flat_xn[:, 0:DC * D].rearrange("p (c n) -> p c n", c=DC)
        aw_row = flat_xn[:, 512:1024]
        bv_row = flat_xn[:, 1024:1280]
        bk_rows = flat_xn[:, 1280:1280 + K * D]
        WARM_UP = 26
        N_LOGIT, N_REST = 5, 5

        block = ctx.enter_context(nc.Block())

        @block.sync
        def _(sp):
            def load_xt(f, c):
                if has_prior(f - 1):
                    sp.wait_ge(w_part_done, nth(f - 2, SU, SU - RING + c + 1))
                elif f == 1:
                    sp.wait_ge(xt_lo_done, nth(f - 1, XC, c + 1))
                sp.dma_start(stage[:, c, :].rearrange("p (c n) -> p c n", c=DC),
                             xT[f].rearrange("(c p) n -> p c n", p=P)[:, :, c * XCW:(c + 1) * XCW])\
                    .then_inc(s_xt[c], 16)

            def load_adj_a(f, u):
                if u >= RING:
                    sp.wait_ge(alpha_done, nth(f, UNITS, u - RING + 1))
                elif has_prior(f):
                    sp.wait_ge(alpha_done, nth(f - 1, UNITS, UNITS + u - RING + 1))
                h, jt = divmod(u, NT)
                sp.dma_start(adj_a[:, u % RING, :],
                             adjT[f].rearrange("(j p) i -> p j i", p=P)[:, jt, h * HALF:(h + 1) * HALF])\
                    .then_inc(s_adja[u % RING], 16)

            def load_adj_s(g, front, v):
                if v >= RING:
                    sp.wait_ge(w_part_done, nth(g, SU, v - RING + 1))
                elif front:
                    sp.wait_ge(xt_lo_done, nth(g + 1, XC, v + 1))
                else:
                    sp.wait_ge(w_part_done, nth(g - 1, SU, SU - RING + v + 1))
                h, it = divmod(v, NT)
                sp.dma_start(stage[:, v % RING, :],
                             adj[g].rearrange("(n p) j -> p n j", p=P)[:, it, h * HALF:(h + 1) * HALF])\
                    .then_inc(s_adjs[v % RING], 16)

            def load_weights(group, sem_):
                for dst, src in group:
                    sp.dma_start(dst, src.rearrange("(c p) n -> p c n", p=P)).then_inc(sem_, 16)

            load_weights(((wv_nat, Wv), (w2_raw, Wk[2])), s_par_logit)
            sp.dma_start(aw_row, aw.rearrange("a o -> o a").to_broadcast([P, 2 * D])).then_inc(s_par_logit, 16)
            sp.dma_start(bv_row, bv.rearrange("(o a) -> o a", o=1).to_broadcast([P, D])).then_inc(s_par_logit, 16)
            sp.dma_start(ab_col[:, :], ab.rearrange("(o a) -> o a", o=1).to_broadcast([P, 1])).then_inc(s_par_logit, 16)

            def slot(s, front, back, tail):
                f, g, t = s, s - 1, s - 2
                if front:
                    for c in range(XC):
                        load_xt(f, c)
                    if not has_prior(f):
                        load_weights(((w10_raw[:, :, 0:D], Wk[1]), (w10_raw[:, :, D:2 * D], Wk[0]),
                                      (wqk_raw, WqkT), (wvT_raw, WvT)), s_par_rest)
                        sp.dma_start(bk_rows, bk.rearrange("(o k) d -> o (k d)", o=1).to_broadcast([P, K * D]))\
                            .then_inc(s_par_rest, 16)
                    for u in range(RING):
                        load_adj_a(f, u)
                if back:
                    for v in range(RING):
                        load_adj_s(g, front, v)
                for h in range(NH):
                    tiles = slice(h * TPH, (h + 1) * TPH)
                    if tail:
                        sp.wait_ge(out_done, nth(t, NT, (h + 1) * TPH))
                        sp.dma_start(out[t].rearrange("(n p) d -> p n d", p=P)[:, tiles, :],
                                     v_sb[:, tiles, :]).then_inc(s_out[h], 16)
                    if back:
                        if not tail:
                            sp.wait_ge(s_w2_ready, 1)
                            sp.wait_ge(s_bias, 2)
                        sp.dma_start(xn[:, tiles, :],
                                     x[g].rearrange("(n p) d -> p n d", p=P)[:, tiles, :]).then_inc(s_xn[h], 16)
                    if front and h == 0:
                        load_adj_a(f, RING)
                if front:
                    for u in range(RING + 1, UNITS):
                        load_adj_a(f, u)
                if back:
                    for v in range(RING, SU):
                        load_adj_s(g, front, v)

            run_slots(sp, slot)
            for h in range(NH):
                sp.wait_ge(s_out[h], nth(B - 1, 16, 16))

        @block.gpsimd
        def _(pool):
            TT = nc.gpsimd.tensor_tensor
            nc.gpsimd.memset(ident[:, :], 0.0).then_inc(s_id0, 1)
            pool.wait_ge(s_id0, 1)
            nc.gpsimd.affine_select(out=ident[:, :], in_=ident[:, :], compare_op=ALU.not_equal, fill=1.0,
                                    base=0, pattern=[[-1, P]], channel_multiplier=1).then_inc(s_const, 1)
            nc.gpsimd.memset(neg_half[:, :], -0.5).then_inc(s_const, 1)

            def a_lo_unit(f, g, back, u):
                h, jt = divmod(u, NT)
                if back and jt == 0:
                    pool.wait_ge(hop_done, nth(g, 2 * NT, NT + TPH * (h + 1)))
                if not has_prior(f):
                    pool.wait_ge(a_hi_act, u + 1)
                elif u in HI_ON_DVE:
                    pool.wait_ge(a_hi_dve, nth(f - 1, N_DVE, u - HI_ON_DVE[0] + 1))
                else:
                    pool.wait_ge(a_hi_act, nth(f, UNITS - N_DVE, u + 1 + (N_DVE if u < HI_ON_DVE[0] else 0)))
                cols = slice(h * HALF, (h + 1) * HALF)
                TT(a_lo[:, jt, cols], unit[:, u % UR, :], a_hi[:, jt, cols].bitcast(F32), ALU.subtract)\
                    .then_inc(a_lo_done, 1)

            def add_bias(f, nt):
                pool.wait_ge(xw_copied, nth(f, NT, nt + 1))
                TT(xw[:, nt, D:2 * D], xw[:, nt, D:2 * D], bias_row[:, :], ALU.add).then_inc(bias_done, 1)

            def norm_scale(b, h, var, rs, sh):
                half = slice(TPH * h, TPH * h + TPH)
                pool.wait_ge(var, nth(b, 2, h + 1))
                TT(rstd[:, half], var_e[:, half], neg_half[:, :], ALU.pow).then_inc(rs, 1)
                pool.wait_ge(rs, nth(b, 2, h + 1))
                TT(shift[:, half], n_mean[:, half], rstd[:, half], ALU.mult).then_inc(sh, 1)

            def bias_sum():
                pool.wait_ge(s_par_rest, N_REST * 16)
                TT(bias_row[:, :], bk_rows[:, 0:D], bk_rows[:, D:2 * D], ALU.add).then_inc(s_bias, 1)
                pool.wait_ge(s_bias, 1)
                TT(bias_row[:, :], bias_row[:, :], bk_rows[:, 2 * D:3 * D], ALU.add).then_inc(s_bias, 1)
                pool.wait_ge(s_bias, 2)

            def weights_qkv_lo():
                pool.wait_ge(s_wqkv_hi, 1)
                for raw, hi, lo in ((wqk_raw[:, :, 0:E], wqq_hi[:, :, 0:E], wqq_lo[:, :, 0:E]),
                                    (wqk_raw[:, :, 0:E], wqq_hi[:, :, E:2 * E], wqq_lo[:, :, E:2 * E]),
                                    (wqk_raw[:, :, E:2 * E], wkk_hi[:, :, 0:E], wkk_lo[:, :, 0:E]),
                                    (wqk_raw[:, :, E:2 * E], wkk_hi[:, :, E:2 * E], wkk_lo[:, :, E:2 * E]),
                                    (wvT_raw, wv_hi[:, :, :], wv_lo[:, :, :])):
                    last = TT(lo, raw, hi.bitcast(F32), ALU.subtract)
                last.then_inc(s_wqkv_ready, 1)

            def slot(s, front, back, tail):
                f, g, t = s, s - 1, s - 2
                if front:
                    for c in range(XC):
                        pool.wait_ge(xt_hi_done, nth(f, XC, c + 1))
                        cols = slice(c * XCW, (c + 1) * XCW)
                        TT(xt_lo[:, :, cols], stage[:, c, :].rearrange("p (c n) -> p c n", c=DC),
                           xt_hi[:, :, cols].bitcast(F32), ALU.subtract).then_inc(xt_lo_done, 1)
                    if not has_prior(f):
                        bias_sum()
                for it in range(NT):
                    if back:
                        pool.wait_ge(z_hi_done, nth(g, NT, it + 1))
                        TT(z_cat[:, it, D:2 * D], xw[:, it, 0:D], z_cat[:, it, 0:D].bitcast(F32), ALU.subtract)\
                            .then_inc(z_lo_done, 1)
                    if tail and it in (4, 6):
                        norm_scale(t, it // 2 - 2, var2_done, rstd2_done, shift2_done)
                if back and not tail:
                    weights_qkv_lo()
                for it in range(NT):
                    if back:
                        if it % TPH == 0:
                            pool.wait_ge(s_xn[it // TPH], nth(g, 16, 16))
                        pool.wait_ge(relu_done, nth(g, NT, it + 1))
                        TT(xn[:, it, :], xw[:, it, D:2 * D], xn[:, it, :], ALU.add).then_inc(res_done, 1)
                    if back and it == 5:
                        norm_scale(g, 0, var_done, rstd_done, shift_done)
                    if front:
                        for u in LO_AT_HOP2[it]:
                            a_lo_unit(f, g, back, u)
                if back:
                    norm_scale(g, 1, var_done, rstd_done, shift_done)
                elif front:
                    for u in range(LO_LEFT, UNITS):
                        a_lo_unit(f, g, back, u)
                    for nt in range(NT):
                        add_bias(f, nt)
                if front and back:
                    for u in range(LO_LEFT, 10):
                        a_lo_unit(f, g, back, u)
                    for u in range(10, 14):
                        add_bias(f, 2 * (u - 10))
                        a_lo_unit(f, g, back, u)
                        add_bias(f, 2 * (u - 10) + 1)
                    a_lo_unit(f, g, back, 14)
                    a_lo_unit(f, g, back, 15)

            run_slots(pool, slot)

        @block.scalar
        def _(act):
            act.wait_ge(s_par_logit, N_LOGIT * 16)
            nc.scalar.copy(w2_hi[:, :, 0:D], w2_raw).then_inc(s_w2_hi, 1)

            def w10_hi_copy():
                act.wait_ge(s_par_rest, N_REST * 16)
                nc.scalar.copy(w10_hi[:, :, :], w10_raw).then_inc(s_w10_hi, 1)

            def weights_qkv_hi():
                nc.scalar.copy(wqq_hi[:, :, 0:E], wqk_raw[:, :, 0:E])
                nc.scalar.copy(wqq_hi[:, :, E:2 * E], wqk_raw[:, :, 0:E])
                nc.scalar.copy(wkk_hi[:, :, 0:E], wqk_raw[:, :, E:2 * E])
                nc.scalar.copy(wkk_hi[:, :, E:2 * E], wqk_raw[:, :, E:2 * E])
                nc.scalar.copy(wv_hi[:, :, :], wvT_raw).then_inc(s_wqkv_hi, 1)

            def si_slope_half(f, h):
                if h == 0 and has_prior(f):
                    act.wait_ge(lrelu_done, nth(f - 1, UNITS, UNITS))
                act.wait_ge(si_done, nth(f, NH, h + 1))
                nc.scalar.mul(si_slope[:, h * HALF:(h + 1) * HALF], si_b[h][:, :], SLOPE).then_inc(si_slope_done, 1)

            def exp_unit(f, u):
                act.wait_ge(lrelu_done, nth(f, UNITS, u + 1))
                jt = u % NT
                nc.scalar.activation(unit[:, u % UR, :], unit[:, u % UR, :], ACT.Exp, bias=logit[:, jt, 1:2])\
                    .then_inc(exp_done, 1)

            def a_hi_unit(f, g, back, u):
                h, jt = divmod(u, NT)
                if back and jt == 0:
                    act.wait_ge(hop_done, nth(g, 2 * NT, NT + TPH * (h + 1)))
                act.wait_ge(alpha_done, nth(f, UNITS, u + 1))
                nc.scalar.copy(a_hi[:, jt, h * HALF:(h + 1) * HALF], unit[:, u % UR, :]).then_inc(a_hi_act, 1)

            def normalise_out(t, n):
                if n % TPH == 0:
                    act.wait_ge(shift2_done, nth(t, 2, n // TPH + 1))
                nc.scalar.activation(v_sb[:, n, :], xn[:, n, :], ACT.Identity, bias=shift[:, n:n + 1],
                                     scale=rstd[:, n:n + 1]).then_inc(out_done, 1)

            def xw_copy(f, g, back, nt):
                if back:
                    act.wait_ge(res_done, nth(g, NT, nt + 1))
                act.wait_ge(xw10_done, nth(f, NT, nt + 1))
                nc.scalar.copy(xw[:, nt, :], bank(U_XW10 + nt)[:, :]).then_inc(xw_copied, 1)

            def x1t_hi_copy(g, i):
                act.wait_ge(x1t_done, nth(g, 4, i + 1))
                if i == 0:
                    act.wait_ge(hop_done, nth(g, 2 * NT, 2 * NT))
                nc.scalar.copy(x1t_hi[:, :, 256 * i:256 * i + 256],
                               hop[i % 2][:, :].rearrange("p (c n) -> p c n", c=DC)).then_inc(x1t_hi_done, 1)

            def qk_hi_copy(g, m):
                act.wait_ge(qk_done, nth(g, 2 * NH, m + 1))
                if m == 0 and has_prior(g):
                    act.wait_ge(s_done, nth(g - 1, SU, SU))
                h, dst = m // 2, (q_hi, k_cat)[m % 2]
                nc.scalar.copy(dst[:, h * HALF:(h + 1) * HALF], bank(U_QK + m)[:, :]).then_inc(qk_hi_done, 1)

            def slot(s, front, back, tail):
                f, g, t = s, s - 1, s - 2
                if front:
                    if has_prior(f):
                        act.wait_ge(xw10_done, nth(f - 1, NT, NT))
                    for c in range(XC):
                        act.wait_ge(s_xt[c], nth(f, 16, 16))
                        nc.scalar.copy(xt_hi[:, :, c * XCW:(c + 1) * XCW],
                                       stage[:, c, :].rearrange("p (c n) -> p c n", c=DC)).then_inc(xt_hi_done, 1)
                for it in range(NT):
                    if back:
                        if it == 0 and has_prior(g):
                            act.wait_ge(v_done, nth(g - 1, NT, NT))
                        act.wait_ge(z_done, nth(g, NT, it + 1))
                        nc.scalar.copy(z_cat[:, it, 0:D], xw[:, it, 0:D]).then_inc(z_hi_done, 1)
                    if tail and it == 2:
                        act.wait_ge(nmax_done, nth(t, 1, 1))
                        nc.scalar.activation(e_col[:, :], w_col[:, :], ACT.Exp, bias=n_max[:, :], scale=SCALE,
                                             accum_out=e_sum[:, :]).then_inc(p_exp_done, 1)
                    if tail and it == 5:
                        for n in range(TPH):
                            normalise_out(t, n)
                if front:
                    for nt in range(NT):
                        act.wait_ge(xw2_done, nth(f, NT, nt + 1))
                        nc.scalar.copy(y_cat[:, nt, 0:D], bank(U_XW2 + nt)[:, 0:D]).then_inc(y_hi_done, 1)
                    si_slope_half(f, 0)
                    if not back:
                        si_slope_half(f, 1)
                        w10_hi_copy()
                if tail:
                    normalise_out(t, TPH)
                    normalise_out(t, TPH + 1)
                if front:
                    exp_unit(f, 0)
                    exp_unit(f, 1)
                if tail:
                    normalise_out(t, NT - 2)
                    if not back:
                        normalise_out(t, NT - 1)
                if front and not back:
                    for u in range(UNITS):
                        a_hi_unit(f, g, back, u)
                        if u + 2 < UNITS:
                            exp_unit(f, u + 2)
                        if u in XW_AT_FIRST:
                            xw_copy(f, g, back, XW_AT_FIRST.index(u))
                    weights_qkv_hi()
                if not back:
                    return
                for it in range(NT):
                    act.wait_ge(h_done, nth(g, NT, it + 1))
                    nc.scalar.activation(xw[:, it, D:2 * D], xw[:, it, D:2 * D], ACT.Relu).then_inc(relu_done, 1)
                    if front:
                        for u in UNITS_AT_HOP2[it]:
                            exp_unit(f, u + 2)
                        if it == 1:
                            si_slope_half(f, 1)
                    if tail and it == 0:
                        normalise_out(t, NT - 1)
                    if front:
                        for u in LO_AT_HOP2[it]:
                            a_hi_unit(f, g, back, u)
                if front:
                    xw_copy(f, g, back, 0)
                    a_hi_unit(f, g, back, 5)
                    exp_unit(f, 12)
                    xw_copy(f, g, back, 1)
                    a_hi_unit(f, g, back, 6)
                    xw_copy(f, g, back, 2)
                    a_hi_unit(f, g, back, 7)
                    xw_copy(f, g, back, 3)
                    exp_unit(f, 13)
                    xw_copy(f, g, back, 4)
                x1t_hi_copy(g, 0)
                x1t_hi_copy(g, 1)
                if front:
                    xw_copy(f, g, back, 5)
                    exp_unit(f, 14)
                    xw_copy(f, g, back, 6)
                    xw_copy(f, g, back, 7)
                else:
                    qk_hi_copy(g, 0)
                x1t_hi_copy(g, 2)
                x1t_hi_copy(g, 3)
                if front:
                    exp_unit(f, 15)
                    qk_hi_copy(g, 0)
                qk_hi_copy(g, 1)
                qk_hi_copy(g, 2)
                qk_hi_copy(g, 3)
                if front:
                    a_hi_unit(f, g, back, 14)
                for j in range(NT):
                    act.wait_ge(v_done, nth(g, NT, j + 1))
                    if j % TPH == 0 and tail:
                        act.wait_ge(s_out[j // TPH], nth(t, 16, 16))
                    nc.scalar.copy(v_sb[:, j, :], bank(U_V + j)[:, 0:D]).then_inc(v_copied, 1)
                    if front and j == 1:
                        a_hi_unit(f, g, back, 15)

            run_slots(act, slot)

        @block.vector
        def _(dve):
            V = nc.vector
            n_set = [0]

            def step(ins):
                n_set[0] += 1
                ins.then_inc(s_setv, 1)
                dve.wait_ge(s_setv, n_set[0])

            step(V.memset(ones[:, :], 1.0))
            for nt in range(NT):
                V.tensor_copy(y_cat[:, nt, D:YL], ones[:, 0:2])
            dve.wait_ge(s_par_logit, N_LOGIT * 16)
            for a in range(2):
                aw_half = aw_row[:, a * D:(a + 1) * D]
                for c in range(DC):
                    V.scalar_tensor_tensor(unit[:, a, c * D:(c + 1) * D], wv_nat[:, c, :], 1.0, aw_half, ALU.mult,
                                           ALU.mult, accum_out=u_cols[:, a, c:c + 1])
                V.scalar_tensor_tensor(unit[:, 2, a * D:(a + 1) * D], bv_row, 1.0, aw_half, ALU.mult,
                                       ALU.mult, accum_out=c_parts[:, a:a + 1])
            step(V.tensor_copy(c_parts[:, 2:3], ab_col[:, :]))
            V.tensor_scalar(u_log[:, :, 0], u_cols[:, 0, :], 1.0 - SLOPE, None, ALU.mult)
            V.tensor_scalar(u_log[:, :, 1], u_cols[:, 0, :], SLOPE, None, ALU.mult)
            V.tensor_copy(u_log[:, :, 2], u_cols[:, 1, :])
            V.tensor_copy(u_log[:, :, 3], u_cols[:, 1, :])
            V.memset(c_add[:, :], 0.0)
            step(V.tensor_reduce(c_col[:, :], c_parts[:, :], AX_X, ALU.add))
            V.tensor_scalar(c_add[:, 0:1], c_col[:, :], 1.0 - SLOPE, None, ALU.mult)
            V.tensor_scalar(c_add[:, 1:2], c_col[:, :], SLOPE, None, ALU.mult)
            step(V.tensor_copy(w2_hi[:, :, D:D + LC], u_log[:, :, :]))
            V.tensor_tensor(w2_lo[:, :, D:D + LC], u_log[:, :, :], w2_hi[:, :, D:D + LC].bitcast(F32), ALU.subtract)
            dve.wait_ge(s_w2_hi, 1)
            V.tensor_tensor(w2_lo[:, :, 0:D], w2_raw, w2_hi[:, :, 0:D].bitcast(F32), ALU.subtract)\
                .then_inc(s_w2_ready, 1)
            dve.wait_ge(s_w2_ready, 1)

            def lrelu_unit(f, u):
                h, jt = divmod(u, NT)
                if u >= UR:
                    dve.wait_ge(a_lo_done, nth(f, UNITS, u - UR + 1))
                elif u == 0 and has_prior(f):
                    dve.wait_ge(a_lo_done, nth(f - 1, UNITS, UNITS))
                if u == 0:
                    dve.wait_ge(y_lo_done, nth(f, NT, NT))
                if jt == 0:
                    dve.wait_ge(si_slope_done, nth(f, NH, h + 1))
                V.scalar_tensor_tensor(unit[:, u % UR, :], si_b[h][:, :], logit[:, jt, 0:1],
                                       si_slope[:, h * HALF:(h + 1) * HALF], ALU.add, ALU.max)\
                    .then_inc(lrelu_done, 1)

            def alpha_unit(f, u):
                dve.wait_ge(exp_done, nth(f, UNITS, u + 1))
                dve.wait_ge(s_adja[u % RING], nth(f, 16 * (UNITS // RING), 16 * (u // RING + 1)))
                V.tensor_tensor(unit[:, u % UR, :], unit[:, u % UR, :], adj_a[:, u % RING, :], ALU.mult)\
                    .then_inc(alpha_done, 1)
                if u + 2 < UNITS:
                    lrelu_unit(f, u + 2)

            def a_hi_unit(f, g, u):
                h, jt = divmod(u, NT)
                if u == HI_ON_DVE[0]:
                    dve.wait_ge(hop_done, nth(g, 2 * NT, 2 * NT))
                dve.wait_ge(alpha_done, nth(f, UNITS, u + 1))
                V.tensor_copy(a_hi[:, jt, h * HALF:(h + 1) * HALF], unit[:, u % UR, :]).then_inc(a_hi_dve, 1)

            def normalise_x1(g, h):
                dve.wait_ge(shift_done, nth(g, 2, h + 1))
                for n in range(TPH * h, TPH * h + TPH):
                    V.tensor_scalar(xn[:, n, :], xn[:, n, :], rstd[:, n:n + 1], shift[:, n:n + 1],
                                    ALU.mult, ALU.add).then_inc(x1_done, 1)

            def x1t_lo_part(g, i):
                cols = slice(256 * i, 256 * i + 256)
                dve.wait_ge(x1t_hi_done, nth(g, 4, i + 1))
                V.tensor_tensor(x1t_lo[:, :, cols], hop[i % 2][:, :].rearrange("p (c n) -> p c n", c=DC),
                                x1t_hi[:, :, cols].bitcast(F32), ALU.subtract).then_inc(x1t_lo_done, 1)

            def qk_lo_part(g, m):
                h = m // 2
                cols = slice(h * HALF, (h + 1) * HALF)
                dst, hi, rows = ((q_lo, q_hi, slice(0, E)), (k_cat, k_cat, slice(E, 2 * E)))[m % 2]
                dve.wait_ge(qk_hi_done, nth(g, 2 * NH, m + 1))
                V.tensor_tensor(dst[rows, cols], bank(U_QK + m)[rows, :], hi[rows, cols].bitcast(F32),
                                ALU.subtract).then_inc(qk_lo_done, 1)

            def score_unit(g, u):
                h, it = divmod(u, NT)
                dve.wait_ge(s_done, nth(g, SU, u + 1))
                dve.wait_ge(s_adjs[u % RING], nth(g, 16 * (SU // RING), 16 * (u // RING + 1)))
                V.scalar_tensor_tensor(stage[:, u % RING, :], score[u % 4][:, :], 1.0, stage[:, u % RING, :],
                                       ALU.mult, ALU.mult, accum_out=w_part[:, it, h:h + 1])\
                    .then_inc(w_part_done, 1)

            def moments(b, h, aggr, var):
                half = slice(TPH * h, TPH * h + TPH)
                V.memset(var_e[:, half], EPS)
                for n in range(TPH * h, TPH * h + TPH):
                    V.bn_aggr(mv[:, n, :], stats[:, n, :]).then_inc(aggr, 1)
                dve.wait_ge(aggr, nth(b, NT, TPH * h + TPH))
                V.tensor_scalar(n_mean[:, half], mv[:, half, 0], -1.0, None, ALU.mult)
                V.tensor_tensor(var_e[:, half], mv[:, half, 1], var_e[:, half], ALU.add).then_inc(var, 1)

            def row_sum(g, it):
                dve.wait_ge(hop_done, nth(g, 2 * NT, it + 1))
                V.tensor_scalar(rsum[:, it:it + 1], hop[it % 2][:, D:D + 1], ROW_EPS, None, ALU.add)\
                    .then_inc(rsum_done, 1)

            def row_inverse(g, it):
                dve.wait_ge(rsum_done, nth(g, NT, it + 1))
                V.reciprocal(rinv[:, it:it + 1], rsum[:, it:it + 1]).then_inc(rinv_done, 1)

            def z_tile(g, it):
                if it == 0:
                    dve.wait_ge(xw_copied, nth(g, NT, NT))
                dve.wait_ge(rinv_done, nth(g, NT, it + 1))
                V.scalar_tensor_tensor(xw[:, it, 0:D], hop[it % 2][:, 0:D], rinv[:, it:it + 1],
                                       xw[:, it, 0:D], ALU.mult, ALU.add).then_inc(z_done, 1)

            def y2_tile(t, n):
                V.scalar_tensor_tensor(xn[:, n, :], v_sb[:, n, :], p_col[:, n:n + 1], xn[:, n, :],
                                       ALU.mult, ALU.add).then_inc(y2_done, 1)

            def y2_stats(t, n):
                dve.wait_ge(y2_done, nth(t, NT, n + 1))
                V.bn_stats(stats[:, n, :], xn[:, n, :]).then_inc(stats2_done, 1)

            def x1_stats(g, n):
                dve.wait_ge(res_done, nth(g, NT, n + 1))
                V.bn_stats(stats[:, n, :], xn[:, n, :]).then_inc(stats_done, 1)

            def slot(s, front, back, tail):
                f, g, t = s, s - 1, s - 2
                for it in range(NT):
                    if tail and it == 3:
                        dve.wait_ge(tot_done, nth(t, 1, 1))
                        V.reciprocal(t_inv[:, :], p_tot).then_inc(tinv_done, 1)
                        dve.wait_ge(tinv_done, nth(t, 1, 1))
                        V.tensor_scalar(p_col[:, :], e_col[:, :], t_inv[:, :], None, ALU.mult).then_inc(p_done, 1)
                        dve.wait_ge(p_done, nth(t, 1, 1))
                    y2_step = tail and 3 <= it < 7
                    z_step = back and (tail or it >= 2)
                    if z_step:
                        row_sum(g, it)
                    if y2_step:
                        y2_tile(t, 2 * it - 6)
                    if z_step:
                        row_inverse(g, it)
                    if y2_step:
                        y2_tile(t, 2 * it - 5)
                    if z_step:
                        z_tile(g, it)
                    if y2_step:
                        y2_stats(t, 2 * it - 6)
                        y2_stats(t, 2 * it - 5)
                        if it % 2 == 0:
                            dve.wait_ge(stats2_done, nth(t, NT, 2 * it - 4))
                            moments(t, it // 2 - 2, aggr2_done, var2_done)
                    if tail and it == 0:
                        dve.wait_ge(maxT_done, nth(t, 1, 1))
                        V.tensor_reduce(g_max[:, :], p_maxT, AX_X, ALU.max).then_inc(gmax_done, 1)
                    if tail and it == 1:
                        dve.wait_ge(maxB_done, nth(t, 1, 1))
                        V.tensor_scalar(n_max[:, :], p_maxB, -SCALE, None, ALU.mult).then_inc(nmax_done, 1)
                if front:
                    for nt in range(NT):
                        b = bank(U_XW2 + nt)
                        dve.wait_ge(y_hi_done, nth(f, NT, nt + 1))
                        V.tensor_tensor(logit[:, nt, :], b[:, D:D + LC], c_add[:, :], ALU.add)
                        V.tensor_tensor(y_cat[:, nt, YL:YL + D], b[:, 0:D], y_cat[:, nt, 0:D].bitcast(F32),
                                        ALU.subtract).then_inc(y_lo_done, 1)
                    lrelu_unit(f, 0)
                    lrelu_unit(f, 1)
                    if not has_prior(f):
                        dve.wait_ge(s_w10_hi, 1)
                        V.tensor_tensor(w10_lo[:, :, :], w10_raw, w10_hi[:, :, :].bitcast(F32), ALU.subtract)\
                            .then_inc(s_w10_ready, 1)
                for it in range(NT):
                    if back:
                        if it == 0:
                            dve.wait_ge(bias_done, nth(g, NT, NT))
                        dve.wait_ge(hop_done, nth(g, 2 * NT, NT + it + 1))
                        V.scalar_tensor_tensor(xw[:, it, D:2 * D], hop[it % 2][:, 0:D], rinv[:, it:it + 1],
                                               xw[:, it, D:2 * D], ALU.mult, ALU.add).then_inc(h_done, 1)
                    if front:
                        for u in UNITS_AT_HOP2[it]:
                            alpha_unit(f, u)
                    if back and it:
                        x1_stats(g, it - 1)
                    if back and it == 4:
                        dve.wait_ge(stats_done, nth(g, NT, TPH))
                        moments(g, 0, aggr_done, var_done)
                    if back and not front and it == 6:
                        normalise_x1(g, 0)
                if front and not back:
                    for u in range(10, UNITS):
                        alpha_unit(f, u)
                        if u in (12, 14):
                            it = u // 2 - 6
                            row_sum(f, it)
                            row_inverse(f, it)
                            z_tile(f, it)
                if not back:
                    return
                if front:
                    alpha_unit(f, 10)
                    a_hi_unit(f, g, 8)
                x1_stats(g, NT - 1)
                dve.wait_ge(stats_done, nth(g, NT, NT))
                moments(g, 1, aggr_done, var_done)
                if front:
                    normalise_x1(g, 0)
                    a_hi_unit(f, g, 9)
                    alpha_unit(f, 11)
                    a_hi_unit(f, g, 10)
                    alpha_unit(f, 12)
                    normalise_x1(g, 1)
                    x1t_lo_part(g, 0)
                    x1t_lo_part(g, 1)
                else:
                    x1t_lo_part(g, 0)
                    x1t_lo_part(g, 1)
                    normalise_x1(g, 1)
                if front:
                    a_hi_unit(f, g, 11)
                    alpha_unit(f, 13)
                x1t_lo_part(g, 2)
                x1t_lo_part(g, 3)
                if front:
                    a_hi_unit(f, g, 12)
                    alpha_unit(f, 14)
                qk_lo_part(g, 0)
                qk_lo_part(g, 1)
                if front:
                    a_hi_unit(f, g, 13)
                    alpha_unit(f, 15)
                qk_lo_part(g, 2)
                score_unit(g, 0)
                score_unit(g, 1)
                qk_lo_part(g, 3)
                for u in range(2, SU):
                    score_unit(g, u)
                dve.wait_ge(w_part_done, nth(g, SU, SU))
                V.tensor_tensor(w_col[:, :], w_part[:, :, 0], w_part[:, :, 1], ALU.add).then_inc(w_col_done, 1)
                dve.wait_ge(w_col_done, nth(g, 1, 1))
                V.tensor_reduce(w_max[:, :], w_col[:, :], AX_X, ALU.max).then_inc(wmax_done, 1)

            run_slots(dve, slot)

        @block.tensor
        def _(pe):
            mm = nc.tensor.matmul

            def mm3(o, l_hi, l_lo, r_hi, r_lo, first, last):
                mm(o, l_hi, r_hi, start=first, stop=False)
                mm(o, l_hi, r_lo, start=False, stop=False)
                return mm(o, l_lo, r_hi, start=False, stop=last)

            pe.wait_ge(s_const, 1)
            for _ in range(WARM_UP):
                mm(misc[:, 384:384 + P], ident[:, :], ident[:, :], start=True, stop=True)
            pe.wait_ge(s_w2_ready, 1)

            def xw2_tile(f, nt):
                if nt % (NT // XC) == 0:
                    pe.wait_ge(xt_lo_done, nth(f, XC, nt // (NT // XC) + 1))
                if nt >= 3:
                    pe.wait_ge(y_lo_done, nth(f, NT, nt - 2))
                elif nt == 0 and has_prior(f - 1):
                    pe.wait_ge(v_copied, nth(f - 2, NT, NT))
                elif nt == 0 and f == 1:
                    pe.wait_ge(xw_copied, nth(f - 1, NT, NT))
                rows = slice(nt * P, (nt + 1) * P)
                for c in range(DC):
                    last = mm3(bank(U_XW2 + nt)[:, 0:D + LC], xt_hi[:, c, rows], xt_lo[:, c, rows],
                               w2_hi[:, c, :], w2_lo[:, c, :], c == 0, c == DC - 1)
                last.then_inc(xw2_done, 1)

            def si_rows(f, h):
                pe.wait_ge(y_lo_done, nth(f, NT, (h + 1) * TPH))
                if h == 0 and has_prior(f):
                    pe.wait_ge(lrelu_done, nth(f - 1, UNITS, UNITS))
                    if has_prior(f - 1):
                        pe.wait_ge(w_part_done, nth(f - 2, SU, SU))
                for n in range(TPH):
                    last = nc.tensor.transpose(si_b[h][:, n * P:(n + 1) * P],
                                               logit[:, h * TPH + n, 2:3].to_broadcast([P, P]), ident[:, :])
                last.then_inc(si_done, 1)

            def hop1_tile(g, it):
                if it >= 2:
                    pe.wait_ge(z_done, nth(g, NT, it - 1))
                elif has_prior(g):
                    pe.wait_ge(w_part_done, nth(g - 1, SU, SU - 3 + it))
                o, rows = hop[it % 2], slice(it * P, (it + 1) * P)
                for jt in range(NT):
                    mm(o[:, 0:YL], a_hi[:, jt, rows], y_cat[:, jt, 0:YL], start=(jt == 0), stop=False)
                    mm(o[:, 0:D], a_hi[:, jt, rows], y_cat[:, jt, YL:YL + D], start=False, stop=False)
                    last = mm(o[:, 0:YL], a_lo[:, jt, rows], y_cat[:, jt, 0:YL], start=False, stop=(jt == NT - 1))
                last.then_inc(hop_done, 1)

            def hop2_tile(g, it):
                if it >= 2:
                    pe.wait_ge(h_done, nth(g, NT, it - 1))
                else:
                    pe.wait_ge(z_done, nth(g, NT, NT + it - 1))
                o, rows = hop[it % 2], slice(it * P, (it + 1) * P)
                for jt in range(NT):
                    if it == 0:
                        pe.wait_ge(z_lo_done, nth(g, NT, jt + 1))
                    last = mm3(o[:, 0:D], a_hi[:, jt, rows], a_lo[:, jt, rows], z_cat[:, jt, 0:D],
                               z_cat[:, jt, D:2 * D], jt == 0, jt == NT - 1)
                last.then_inc(hop_done, 1)

            def xw10(f, back, nt):
                if nt < 3:
                    pe.wait_ge(y_lo_done, nth(f, NT, NT - 2 + nt))
                else:
                    pe.wait_ge(xw_copied, nth(f, NT, nt - 2))
                if nt == 0 and not has_prior(f):
                    pe.wait_ge(s_w10_ready, 1)
                rows = slice(nt * P, (nt + 1) * P)
                for c in range(DC):
                    last = mm3(bank(U_XW10 + nt)[:, :], xt_hi[:, c, rows], xt_lo[:, c, rows],
                               w10_hi[:, c, :], w10_lo[:, c, :], c == 0, c == DC - 1)
                last.then_inc(xw10_done, 1)

            def x1_transpose(g, i):
                if i < 2:
                    pe.wait_ge(h_done, nth(g, NT, NT - 1 + i))
                else:
                    pe.wait_ge(x1t_lo_done, nth(g, 4, i - 1))
                pe.wait_ge(x1_done, nth(g, NT, 2 * i + 2))
                b = hop[i % 2]
                for c in range(DC):
                    for j in range(2):
                        last = nc.tensor.transpose(b[:, c * 256 + j * P:c * 256 + (j + 1) * P],
                                                   xn[:, 2 * i + j, c * P:(c + 1) * P], ident[:, :])
                last.then_inc(x1t_done, 1)

            def qk_half(g, front, m):
                if m == 0 and not has_prior(g):
                    pe.wait_ge(s_wqkv_ready, 1)
                if m % 2 == 0:
                    pe.wait_ge(x1t_lo_done, nth(g, 4, m + 2))
                if m == 3:
                    pe.wait_ge(qk_lo_done, nth(g, 2 * NH, 1))
                elif front:
                    pe.wait_ge(xw_copied, nth(g + 1, NT, NT - 2 + m))
                elif m == 0:
                    pe.wait_ge(v_copied, nth(g - 1, NT, NT))
                h, (w_hi, w_lo) = m // 2, ((wqq_hi, wqq_lo), (wkk_hi, wkk_lo))[m % 2]
                cols = slice(h * HALF, (h + 1) * HALF)
                for c in range(DC):
                    last = mm3(bank(U_QK + m)[:, :], w_hi[:, c, :], w_lo[:, c, :], x1t_hi[:, c, cols],
                               x1t_lo[:, c, cols], c == 0, c == DC - 1)
                last.then_inc(qk_done, 1)

            def v_tile(g, j):
                if j < 3:
                    pe.wait_ge(qk_lo_done, nth(g, 2 * NH, j + 2))
                else:
                    pe.wait_ge(v_copied, nth(g, NT, j - 2))
                rows = slice(j * P, (j + 1) * P)
                for c in range(DC):
                    last = mm3(bank(U_V + j)[:, 0:D], x1t_hi[:, c, rows], x1t_lo[:, c, rows],
                               wv_hi[:, c, :], wv_lo[:, c, :], c == 0, c == DC - 1)
                last.then_inc(v_done, 1)

            def score_unit(g, front, u):
                if u < 2:
                    pe.wait_ge(x1t_lo_done, nth(g, 4, 3 + u))
                elif u >= 4:
                    pe.wait_ge(w_part_done, nth(g, SU, u - 3))
                elif u == 2 and front:
                    pe.wait_ge(lrelu_done, nth(g + 1, UNITS, UNITS))
                if u == 0:
                    pe.wait_ge(qk_lo_done, nth(g, 2 * NH, 2))
                if u == TPH:
                    pe.wait_ge(qk_lo_done, nth(g, 2 * NH, 2 * NH))
                h, it = divmod(u, NT)
                rows, cols = slice(it * P, (it + 1) * P), slice(h * HALF, (h + 1) * HALF)
                mm(score[u % 4][:, :], q_hi[:, rows], k_cat[:, cols], start=True, stop=False)
                mm(score[u % 4][:, :], q_lo[:, rows], k_cat[0:E, cols], start=False, stop=True).then_inc(s_done, 1)

            def slot(s, front, back, tail):
                f, g, t = s, s - 1, s - 2
                if back:
                    pe.wait_ge(y_lo_done, nth(g, NT, NT))
                for it in range(NT):
                    if back:
                        if it % TPH == 0:
                            pe.wait_ge(a_lo_done, nth(g, UNITS, NT * (it // TPH + 1)))
                        hop1_tile(g, it)
                    if tail and it == 0:
                        pe.wait_ge(wmax_done, nth(t, 1, 1))
                        nc.tensor.transpose(p_maxT, w_max[:, :], ident[:, :]).then_inc(maxT_done, 1)
                    if tail and it == 1:
                        pe.wait_ge(gmax_done, nth(t, 1, 1))
                        mm(p_maxB, ones[0:1, :], g_max[:, :], start=True, stop=True).then_inc(maxB_done, 1)
                    if tail and it == 3:
                        pe.wait_ge(p_exp_done, nth(t, 1, 1))
                        mm(p_tot, ones[:, :], e_sum[:, :], start=True, stop=True).then_inc(tot_done, 1)
                if front:
                    for nt in range(NT):
                        if nt == NT - 2:
                            si_rows(f, 0)
                        xw2_tile(f, nt)
                    if not back:
                        si_rows(f, 1)
                if back:
                    for it in range(NT):
                        hop2_tile(g, it)
                        if front and it == 0:
                            si_rows(f, 1)
                if front:
                    for nt in range(NT - 2):
                        xw10(f, back, nt)
                if back:
                    x1_transpose(g, 0)
                    x1_transpose(g, 1)
                if front:
                    xw10(f, back, NT - 2)
                    xw10(f, back, NT - 1)
                elif back:
                    qk_half(g, front, 0)
                if back:
                    x1_transpose(g, 2)
                    x1_transpose(g, 3)
                    for m in range(0 if front else 1, 3):
                        qk_half(g, front, m)
                    score_unit(g, front, 0)
                    score_unit(g, front, 1)
                    qk_half(g, front, 3)
                    score_unit(g, front, 2)
                    score_unit(g, front, 3)
                    v_tile(g, 0)
                    for j in range(2, NT):
                        v_tile(g, j - 1)
                        score_unit(g, front, 2 * j)
                        score_unit(g, front, 2 * j + 1)
                    v_tile(g, NT - 1)

            run_slots(pe, slot)


def kernel(x, adj, L0_gnn_Wv, L0_gnn_bv, L0_gnn_aw, L0_gnn_ab, L0_gnn_Wk, L0_gnn_bk, L1_gnn_W_qk, L1_gnn_W_v):
    import numpy as np
    import concourse.bacc as bacc
    from concourse import mybir as mb
    from concourse.bass_utils import run_bass_kernel_spmd as run

    nc = bacc.Bacc("TRN2", target_bir_lowering=False, num_devices=1, dynamic_dma_scratch_size=1024)
    laid = {
        "xT": np.asarray(x).transpose(0, 2, 1), "x": x, "adj": adj, "adjT": np.asarray(adj).transpose(0, 2, 1),
        "Wv": L0_gnn_Wv, "bv": L0_gnn_bv, "aw": L0_gnn_aw, "ab": L0_gnn_ab, "Wk": L0_gnn_Wk, "bk": L0_gnn_bk,
        "WqkT": np.asarray(L1_gnn_W_qk).T, "WvT": np.asarray(L1_gnn_W_v).T,
    }
    arrays, args = {}, []
    for name, a in laid.items():
        a = np.ascontiguousarray(a)
        arrays[f"{name}_dram"] = a
        args.append(nc.dram_tensor(f"{name}_dram", a.shape, mb.dt.from_np(a.dtype), kind="ExternalInput").ap())
    args.append(nc.dram_tensor("out_dram", x.shape, mb.dt.float32, kind="ExternalOutput").ap())
    bass_gnn_pair(nc, *args)
    return run(nc, [arrays], core_ids=[0]).results[0]["out_dram"]
```
